# Optimizing a Trainium2 kernel written in Bass

```python
import numpy as np
import jax
import jax.numpy as jnp

def _softmax(x, axis=-1):
    return jax.nn.softmax(x, axis=axis)

def _gelu(x):
    return jax.nn.gelu(x, approximate=True)

def _silu(x):
    return jax.nn.silu(x)

def _sigmoid(x):
    return jax.nn.sigmoid(x)

def _layernorm(x, axis=-1, eps=1e-05):
    m = jnp.mean(x, axis=axis, keepdims=True)
    v = jnp.var(x, axis=axis, keepdims=True)
    return (x - m) / jnp.sqrt(v + eps)

def _scatter_add(tgt, idx, src, axis=0):
    return tgt.at[idx].add(src)

def _segment_sum(src, seg, n):
    return jax.ops.segment_sum(src, seg, n)
kernel_name = 'mk_adj_resnorm_d2_adj_r2_2b2326'

def setup_inputs(seed: int=0):
    np.random.seed(seed)
    _w = jnp.asarray

    def _rec_inputs():
        import jax
        import jax.numpy as jnp
        _gk = jax.random.key(seed)
        x = -0.000125 + 0.9999 * jax.random.normal(jax.random.fold_in(_gk, 1), (32, 256, 128), jnp.float32)
        _a = jax.random.bernoulli(jax.random.fold_in(_gk, 2), 0.0078125, (256, 256))
        _a = jnp.logical_or(_a, jnp.swapaxes(_a, -1, -2))
        _a = jnp.logical_or(_a, jnp.eye(256, dtype=bool))
        _af = _a.astype(jnp.float32)
        _af = _af * jax.random.uniform(jax.random.fold_in(_gk, 3), (256, 256), jnp.float32, 0.05, 0.000488281)
        adj = _af
        return (x, adj)
    x, adj = _rec_inputs()

    def _L0_gnn_setup():
        import jax, jax.numpy as jnp
        import numpy as np
        B, T, D, H = (64, 1024, 128, 128)
        MAX_SKIP = 4

        def _lstm_last(Wih, Whh, bih, bhh, xs):
            N, _, Hd = xs.shape
            bias = bih + bhh

            def step(carry, x_t):
                h, c = carry
                g = x_t @ Wih.T + h @ Whh.T + bias
                i, f, gg, o = jnp.split(g, 4, axis=-1)
                c = jax.nn.sigmoid(f) * c + jax.nn.sigmoid(i) * jnp.tanh(gg)
                h = jax.nn.sigmoid(o) * jnp.tanh(c)
                return ((h, c), None)
            init = (jnp.zeros((N, Hd), xs.dtype), jnp.zeros((N, Hd), xs.dtype))
            (h_last, _), _ = jax.lax.scan(step, init, jnp.swapaxes(xs, 0, 1))
            return h_last
        key = jax.random.key(seed)
        ks = jax.random.split(key, 8)
        s = 0.05
        x = jax.random.normal(ks[0], (B, T, D), jnp.float32)
        adj = jax.random.uniform(ks[1], (T, T), jnp.float32) / T
        Wg0 = jax.random.normal(ks[2], (D, H), jnp.float32) * s
        bg0 = jnp.zeros((H,), jnp.float32)
        Wg1 = jax.random.normal(ks[3], (H, H), jnp.float32) * s
        bg1 = jnp.zeros((H,), jnp.float32)
        Wih = jax.random.normal(ks[4], (MAX_SKIP, 4 * H, H), jnp.float32) * s
        Whh = jax.random.normal(ks[5], (MAX_SKIP, 4 * H, H), jnp.float32) * s
        bih = jax.random.normal(ks[6], (MAX_SKIP, 4 * H), jnp.float32) * s
        bhh = jax.random.normal(ks[7], (MAX_SKIP, 4 * H), jnp.float32) * s
        return dict(x=x, adj=adj, Wg0=Wg0, bg0=bg0, Wg1=Wg1, bg1=bg1, Wih=Wih, Whh=Whh, bih=bih, bhh=bhh)
    _L0_gnn_all = _L0_gnn_setup()
    _L0_gnn_in = {k: v for k, v in _L0_gnn_all.items() if k in ('Wg0', 'bg0', 'Wg1', 'bg1', 'Wih', 'Whh', 'bih', 'bhh')}
    del _L0_gnn_all

    def _L1_gnn_setup():
        import jax, jax.numpy as jnp
        import numpy as np
        BT, N, D, HEADS, E = (512, 64, 128, 4, 256)
        LRELU_SLOPE = 0.2
        EPS = 1e-08
        key = jax.random.key(seed)
        ks = jax.random.split(key, 8)
        d = D
        return {'H': jax.random.normal(ks[0], (BT, N, d), jnp.float32), 'W_lin': jax.random.normal(ks[1], (d, d), jnp.float32) / np.sqrt(d).astype(np.float32), 'W_val': jax.random.normal(ks[2], (d, d), jnp.float32) / np.sqrt(d).astype(np.float32), 'a': jax.random.normal(ks[3], (HEADS, d // HEADS), jnp.float32), 'W_out': jax.random.normal(ks[4], (d, d), jnp.float32) / np.sqrt(d).astype(np.float32), 'A0': jax.random.uniform(ks[5], (N, N), jnp.float32), 'src': jax.random.randint(ks[6], (E,), 0, N, jnp.int32), 'dst': jax.random.randint(ks[7], (E,), 0, N, jnp.int32)}
    _L1_gnn_all = _L1_gnn_setup()
    _L1_gnn_in = {k: v for k, v in _L1_gnn_all.items() if k in ('W_lin', 'W_val', 'a', 'W_out', 'src', 'dst')}
    del _L1_gnn_all
    return {'x': x, 'adj': adj, 'L0_gnn_Wg0': _L0_gnn_in['Wg0'], 'L0_gnn_bg0': _L0_gnn_in['bg0'], 'L0_gnn_Wg1': _L0_gnn_in['Wg1'], 'L0_gnn_bg1': _L0_gnn_in['bg1'], 'L0_gnn_Wih': _L0_gnn_in['Wih'], 'L0_gnn_Whh': _L0_gnn_in['Whh'], 'L0_gnn_bih': _L0_gnn_in['bih'], 'L0_gnn_bhh': _L0_gnn_in['bhh'], 'L1_gnn_W_lin': _L1_gnn_in['W_lin'], 'L1_gnn_W_val': _L1_gnn_in['W_val'], 'L1_gnn_a': _L1_gnn_in['a'], 'L1_gnn_W_out': _L1_gnn_in['W_out'], 'L1_gnn_src': _L1_gnn_in['src'], 'L1_gnn_dst': _L1_gnn_in['dst']}

def reference(x, adj, L0_gnn_Wg0, L0_gnn_bg0, L0_gnn_Wg1, L0_gnn_bg1, L0_gnn_Wih, L0_gnn_Whh, L0_gnn_bih, L0_gnn_bhh, L1_gnn_W_lin, L1_gnn_W_val, L1_gnn_a, L1_gnn_W_out, L1_gnn_src, L1_gnn_dst):
    import jax
    import jax.numpy as jnp

    def _L0_gnn_ref(x, adj, Wg0, bg0, Wg1, bg1, Wih, Whh, bih, bhh):
        import jax, jax.numpy as jnp
        import numpy as np
        B, T, D, H = (64, 1024, 128, 128)
        MAX_SKIP = 4

        def _lstm_last(Wih, Whh, bih, bhh, xs):
            N, _, Hd = xs.shape
            bias = bih + bhh

            def step(carry, x_t):
                h, c = carry
                g = x_t @ Wih.T + h @ Whh.T + bias
                i, f, gg, o = jnp.split(g, 4, axis=-1)
                c = jax.nn.sigmoid(f) * c + jax.nn.sigmoid(i) * jnp.tanh(gg)
                h = jax.nn.sigmoid(o) * jnp.tanh(c)
                return ((h, c), None)
            init = (jnp.zeros((N, Hd), xs.dtype), jnp.zeros((N, Hd), xs.dtype))
            (h_last, _), _ = jax.lax.scan(step, init, jnp.swapaxes(xs, 0, 1))
            return h_last
        h = jax.nn.relu(jnp.einsum('ts,bsh->bth', adj, x @ Wg0 + bg0))
        h = jax.nn.relu(jnp.einsum('ts,bsh->bth', adj, h @ Wg1 + bg1))
        Bv, Tv, Hd = h.shape
        for p in range(1, MAX_SKIP + 1):
            nw = Tv // p
            wins = h[:, :nw * p, :].reshape(Bv * nw, p, Hd)
            last = _lstm_last(Wih[p - 1], Whh[p - 1], bih[p - 1], bhh[p - 1], wins)
            idx = jnp.arange(nw) * p + (p - 1)
            h = h.at[:, idx, :].set(last.reshape(Bv, nw, Hd))
        return h

    def _L1_gnn_ref(H, W_lin, W_val, a, W_out, A0, src, dst):
        import jax, jax.numpy as jnp
        import numpy as np
        BT, N, D, HEADS, E = (512, 64, 128, 4, 256)
        LRELU_SLOPE = 0.2
        EPS = 1e-08
        bt, n, d = H.shape
        h, dh = a.shape
        Xq = (H @ W_lin.T).reshape(bt, n, h, dh)
        Xv = (H @ W_val.T).reshape(bt, n, h, dh)
        Qs = Xq[:, src]
        Kt = Xq[:, dst]
        e = jnp.einsum('behd,hd->beh', jax.nn.leaky_relu(Qs + Kt, LRELU_SLOPE), a)
        e = e + jnp.log(A0[src, dst] + EPS)[None, :, None]
        e_t = e.transpose(1, 0, 2)
        m = jax.ops.segment_max(e_t, src, num_segments=n)
        ex = jnp.exp(e_t - m[src])
        denom = jax.ops.segment_sum(ex, src, num_segments=n)
        attn = ex / denom[src]
        Vt = Xv[:, dst].transpose(1, 0, 2, 3)
        Y = jax.ops.segment_sum(attn[..., None] * Vt, src, num_segments=n)
        Y = Y.transpose(1, 0, 2, 3).reshape(bt, n, d)
        return Y @ W_out.T
    x = _layernorm(x + _L0_gnn_ref(x, adj, L0_gnn_Wg0, L0_gnn_bg0, L0_gnn_Wg1, L0_gnn_bg1, L0_gnn_Wih, L0_gnn_Whh, L0_gnn_bih, L0_gnn_bhh), axis=-1)
    x = _layernorm(x + _L1_gnn_ref(x, L1_gnn_W_lin, L1_gnn_W_val, L1_gnn_a, L1_gnn_W_out, adj, L1_gnn_src, L1_gnn_dst), axis=-1)
    return x

_drawn_inputs = setup_inputs


def setup_inputs(seed=0):
    import zlib

    import numpy as np

    out = dict(_drawn_inputs(seed))
    spreads = {'L0_gnn_bg0': (0.0, 0.8), 'L0_gnn_bg1': (0.0, 0.8)}
    factors = {'L0_gnn_Wg0': 8.0, 'L0_gnn_Wg1': 8.0, 'L0_gnn_Wih': 8.0, 'L0_gnn_Whh': 8.0}
    for name, (base, spread) in spreads.items():
        noise = np.random.default_rng([zlib.crc32(name.encode()), seed]).standard_normal(out[name].shape)
        drawn = base * np.exp(spread * noise) if base else spread * noise
        out[name] = jnp.asarray(drawn.astype(out[name].dtype))
    for name, factor in factors.items():
        out[name] = (out[name] * factor).astype(out[name].dtype)
    return out
```

```python
from contextlib import ExitStack

import concourse.bass as bass
from concourse import mybir

F32 = mybir.dt.float32
F32R = mybir.dt.float32r
I32 = mybir.dt.int32
ALU = mybir.AluOpType
ACT = mybir.ActivationFunctionType
AX_X = mybir.AxisListType.X

P = 128
BIG = 1e30

GATE_I, GATE_G, GATE_F, GATE_O = range(4)
GATE_ROW = {GATE_I: 0, GATE_F: 1, GATE_G: 2, GATE_O: 3}
GATE_FUNC = {GATE_I: ACT.Sigmoid, GATE_G: ACT.Tanh, GATE_F: ACT.Sigmoid, GATE_O: ACT.Sigmoid}


def lstm_steps(T, skips, job_windows):
    steps = []
    for p in range(1, skips + 1):
        jobs, w = [], 0
        for n in job_windows[p]:
            jobs.append((w, n))
            w += n
        assert w == T // p
        group = {1: 1, 2: 2, 3: len(jobs), 4: len(jobs)}[p]
        for g0 in range(0, len(jobs), group):
            for s in range(p):
                for slot, (w0, nw) in enumerate(jobs[g0:g0 + group]):
                    steps.append(dict(p=p, s=s, w0=w0, nw=nw, slot=slot, group=group,
                                      t0=w0 * p, t1=(w0 + nw) * p))
    full = 0
    for n, st in enumerate(steps):
        st["full"] = full
        full += st["s"] > 0
        need = 0
        for m in range(n):
            o = steps[m]
            if o["s"] == o["p"] - 1 and o["p"] < st["p"] and o["t0"] < st["t1"] and st["t0"] < o["t1"]:
                need = m + 1
        st["need_x"] = need
        st["need_h"] = n - st["group"] + 1
    return steps


def build(nc, x, adjT, adj, Wg0, bg0, Wg1, bg1, WihT, WhhT, bih, bhh, WlinT, WvalT, a, WoutT, src, ends, out):
    NK = x.shape[0]
    B = 2 * NK
    JT = x.shape[3]
    T = JT * P
    D = x.shape[4]
    SK = WihT.shape[1]
    G4 = 4 * D
    E = src.shape[1]
    ET = E // P
    NH, DH = a.shape
    BH = B * NH
    assert (D, T, E, BH, SK) == (P, 2 * P, 2 * P, P, 4)
    PB = 2 * T
    HB = B // 2
    SLOPE, EPS_LN, EPS_LOG = 0.2, 1e-5, 1e-8

    JW = {1: [32] * 8, 2: [32] * 4, 3: [28, 28, 29], 4: [32, 32]}
    STEPS = lstm_steps(T, SK, JW)
    NS = len(STEPS)
    N1 = len(JW[1])
    N2 = len(JW[2])

    stacks = {k: ExitStack() for k in ("all", "weights", "first", "lstm", "edges", "graph", "rows")}

    def sb(stack, name, shape, dt=F32):
        return stacks[stack].enter_context(nc.sbuf_tensor(name, shape, dt))

    xs = [sb("all", f"xs{i}", [P, 2, JT, D]) for i in range(2)]
    adjT_hi = sb("all", "adjT_hi", [P, JT, T], F32R)
    adjT_lo = sb("all", "adjT_lo", [P, JT, T], F32R)
    wg_hi = [sb("all", f"wg{i}_hi", [P, D], F32R) for i in range(2)]
    wg_lo = [sb("all", f"wg{i}_lo", [P, D], F32R) for i in range(2)]
    bias0 = sb("all", "bias0", [P, D], F32R)
    bias1 = sb("all", "bias1", [P, D], F32R)
    ones = sb("all", "ones", [P, P], F32R)
    degree = sb("all", "degree", [P, 2, T], F32R)
    lin_raw = sb("all", "lin_raw", [P, 3, D])
    lin_hi = sb("all", "lin_hi", [P, 3, D], F32R)
    lin_lo = sb("all", "lin_lo", [P, 3, D], F32R)
    head_raw = sb("all", "head_raw", [P, NH])
    head_hi = sb("all", "head_hi", [P, NH], F32R)
    head_lo = sb("all", "head_lo", [P, NH], F32R)
    bias_ih = sb("all", "bias_ih", [P, SK, 4])
    bias_hh = sb("all", "bias_hh", [P, SK, 4])
    bias_gate = sb("all", "bias_gate", [P, SK, 4])
    ident = sb("all", "ident", [P, P])
    iota_row = sb("all", "iota_row", [P, T])
    iota_col = sb("all", "iota_col", [P, JT])
    gather = sb("all", "gather", [P, JT, 2, E], F32R)
    scatter = sb("all", "scatter", [P, ET, T], F32R)
    same = sb("all", "same", [P, E + 1])
    pen = sb("all", "pen", [P, E + 1])
    adj_edge = sb("all", "adj_edge", [P, ET])
    log_adj = sb("all", "log_adj", [P, ET])
    eps_ln = sb("all", "eps_ln", [P, 1])
    hT_hi = sb("all", "hT_hi", [P, T, B], F32R)
    hT_lo = sb("all", "hT_lo", [P, T, B], F32R)

    wl_hi = sb("weights", "wl_hi", [P, 2, SK, G4], F32R)
    wl_lo = sb("weights", "wl_lo", [P, 2, SK, G4], F32R)

    adjT_raw = sb("first", "adjT_raw", [P, JT, T])
    adj_raw = sb("first", "adj_raw", [P, JT, T])
    wg_raw = sb("first", "wg_raw", [P, 2, D])
    b_raw = sb("first", "b_raw", [P, 2, D])
    wl_raw = sb("first", "wl_raw", [P, 2, SK, G4])
    x_hi = [sb("first", f"x_hi{i}", [P, 2, JT, D], F32R) for i in range(2)]
    x_lo = [sb("first", f"x_lo{i}", [P, 2, JT, D], F32R) for i in range(2)]
    z_hi = [sb("first", f"z_hi{i}", [P, PB], F32R) for i in range(2)]
    z_lo = [sb("first", f"z_lo{i}", [P, PB], F32R) for i in range(2)]
    h1_hi = [sb("first", f"h1_hi{i}", [P, PB], F32R) for i in range(2)]
    h1_lo = [sb("first", f"h1_lo{i}", [P, PB], F32R) for i in range(2)]
    u_hi = [sb("first", f"u_hi{i}", [P, 2, JT, D], F32R) for i in range(2)]
    u_lo = [sb("first", f"u_lo{i}", [P, 2, JT, D], F32R) for i in range(2)]
    iota_i = sb("first", "iota_i", [P, T], I32)
    iota_ci = sb("first", "iota_ci", [P, JT], I32)
    ends_i = sb("first", "ends_i", [P, E], I32)
    ends_ci = sb("first", "ends_ci", [P, ET, 2], I32)
    ends_c = sb("first", "ends_c", [P, ET, 2])
    ends_b = sb("first", "ends_b", [P, ET, 2, P])
    key_row = sb("first", "key_row", [P, E])
    key_col = sb("first", "key_col", [P, ET])
    less = sb("first", "less", [P, E])
    rank = sb("first", "rank", [P, ET])
    order = sb("first", "order", [P, ET, E])
    ends_row = sb("first", "ends_row", [P, 2, E])
    ends_sc = sb("first", "ends_sc", [P, ET, 2])
    src_node = sb("first", "src_node", [P, JT, E])
    dst_edge = sb("first", "dst_edge", [P, ET, T])
    stacks["first"].close()

    h_rec_hi = [sb("lstm", f"h_rec_hi{i}", [P, 2, 512], F32R) for i in range(3)]
    h_rec_lo = [sb("lstm", f"h_rec_lo{i}", [P, 2, 512], F32R) for i in range(3)]
    cell = [sb("lstm", f"cell{i}", [P, 2, 512]) for i in range(3)]
    gate = [[sb("lstm", f"gate{g}_{i}", [P, 2, 512]) for i in range(2)] for g in range(4)]
    tanh_c = [sb("lstm", f"tanh_c{i}", [P, 2, 512]) for i in range(2)]
    stacks["lstm"].close()
    stacks["weights"].close()

    values = sb("edges", "values", [P, NK, 2 * ET, D])
    x1 = sb("edges", "x1", [P, NK, 2 * JT, D])
    attn = sb("edges", "attn", [P, B, ET, NH])
    stat = [sb("edges", f"stat{i}", [P, 2 * JT, 6]) for i in range(2)]
    mv = [sb("edges", f"mv{i}", [P, 2 * JT, 2]) for i in range(2)]
    std = [sb("edges", f"std{i}", [P, 2 * JT]) for i in range(2)]
    rstd = [sb("edges", f"rstd{i}", [P, 2 * JT]) for i in range(2)]
    shift = [sb("edges", f"shift{i}", [P, 2 * JT]) for i in range(2)]

    hsum = [sb("graph", f"hsum{i}", [P, 2, T]) for i in range(2)]
    y = [sb("graph", f"y{i}", [P, 2 * JT, D]) for i in range(2)]
    x1_hi = [sb("graph", f"x1_hi{i}", [P, 2 * JT, D], F32R) for i in range(2)]
    x1_lo = [sb("graph", f"x1_lo{i}", [P, 2 * JT, D], F32R) for i in range(2)]
    gv_hi = [sb("graph", f"gv_hi{i}", [P, 2, 2, E], F32R) for i in range(2)]
    gv_lo = [sb("graph", f"gv_lo{i}", [P, 2, 2, E], F32R) for i in range(2)]
    qs = [sb("graph", f"qs{i}", [P, 2, E]) for i in range(2)]
    lr = [sb("graph", f"lr{i}", [P, 2, E]) for i in range(2)]
    lr_hi = [sb("graph", f"lr_hi{i}", [P, 2, E], F32R) for i in range(2)]
    lr_lo = [sb("graph", f"lr_lo{i}", [P, 2, E], F32R) for i in range(2)]
    stacks["graph"].close()

    score_e = sb("rows", "score_e", [P, ET, BH])
    score = sb("rows", "score", [P, E])
    run_f = sb("rows", "run_f", [P, E])
    run_b = sb("rows", "run_b", [P, E])
    top = sb("rows", "top", [P, E])
    ex = sb("rows", "ex", [P, E])
    den = sb("rows", "den", [P, E])
    rden = sb("rows", "rden", [P, E])
    weight = sb("rows", "weight", [P, E])
    vs = [sb("rows", f"vs{i}", [P, 2 * ET, D]) for i in range(2)]
    vs_hi = [sb("rows", f"vs_hi{i}", [P, 2 * ET, D], F32R) for i in range(2)]
    vs_lo = [sb("rows", f"vs_lo{i}", [P, 2 * ET, D], F32R) for i in range(2)]
    yt_hi = [sb("rows", f"yt_hi{i}", [P, 2, T], F32R) for i in range(2)]
    yt_lo = [sb("rows", f"yt_lo{i}", [P, 2, T], F32R) for i in range(2)]
    z = [sb("rows", f"z{i}", [P, 2 * JT, D]) for i in range(2)]
    res = [sb("rows", f"res{i}", [P, 2 * JT, D]) for i in range(2)]
    stacks["rows"].close()
    stacks["edges"].close()

    ps = stacks["all"].enter_context(nc.psum_tensor("ps", [P, 8, 512], F32))
    ps_z = [ps[:, i, :] for i in range(2)]
    ps_h1 = [ps[:, 2 + i, :] for i in range(2)]
    ps_u = [ps[:, 4 + i, :] for i in range(2)]
    ps_h2 = [ps[:, 6 + i, :] for i in range(2)]
    ps_t = [ps[:, i, :] for i in range(2)]
    ps_gv = ps[:, 2:4, :]
    ps_q = [ps[:, 4 + i, :] for i in range(2)]
    ps_v = ps[:, 6, :]
    ps_s = ps[:, 7, :]
    ps_y = [ps[:, 2 + i, :] for i in range(2)]
    ps_o = [ps[:, 4 + i, :] for i in range(2)]

    def sem(name):
        return stacks["all"].enter_context(nc.semaphore(name))

    first_in, small_in, wl_in, row_in, ends_in = (sem(s) for s in ("first_in", "small_in", "wl_in", "row_in", "ends_in"))
    x_in = [sem("x_in0"), sem("x_in1")]
    out_done = [sem("out_done0"), sem("out_done1")]
    consts, iotas, zeroed = sem("consts"), sem("iotas"), sem("zeroed")
    act_prep, dve_prep, pe_prep, pool_prep = (sem(s) for s in ("act_prep", "dve_prep", "pe_prep", "pool_prep"))
    x_high, x_split = sem("x_high"), sem("x_split")
    z_ps, z_high, z_split = sem("z_ps"), sem("z_high"), sem("z_split")
    h1_ps, h1_high, h1_split = sem("h1_ps"), sem("h1_high"), sem("h1_split")
    u_ps, u_high, u_split = sem("u_ps"), sem("u_high"), sem("u_split")
    h2_ps, h2_high, h2_split = sem("h2_ps"), sem("h2_high"), sem("h2_split")
    wl_high, wl_split = sem("wl_high"), sem("wl_split")
    graph_dve, graph_pe = sem("graph_dve"), sem("graph_pe")
    gate_ps = [sem(f"gate_ps{g}") for g in range(4)]
    gate_sb = [sem(f"gate_sb{g}") for g in range(4)]
    in_gate, keep_gate, c_ready, tanh_ready = (sem(s) for s in ("in_gate", "keep_gate", "c_ready", "tanh_ready"))
    h_ready, h_high, h_split = sem("h_ready"), sem("h_high"), sem("h_split")
    hs_ready, t_ps, y_ready, stats_ready, mv_ready = (sem(s) for s in ("hs_ready", "t_ps", "y_ready", "stats_ready", "mv_ready"))
    std_ready, rstd_ready, x1_ready, x1_high, x1_split = (sem(s) for s in ("std_ready", "rstd_ready", "x1_ready", "x1_high", "x1_split"))
    gv_ps, gv_high, gv_split = sem("gv_ps"), sem("gv_high"), sem("gv_split")
    q_ps, q_ready, lr_ready, lr_high, lr_split = (sem(s) for s in ("q_ps", "q_ready", "lr_ready", "lr_high", "lr_split"))
    v_ps, v_ready, s_ps = sem("v_ps"), sem("v_ready"), sem("s_ps")
    soft_dve, soft_act, soft_pe = sem("soft_dve"), sem("soft_act"), sem("soft_pe")
    vs_ready, vs_high, vs_split = sem("vs_ready"), sem("vs_high"), sem("vs_split")
    yt_ps, yt_high, yt_split = sem("yt_ps"), sem("yt_high"), sem("yt_split")
    o_ps, z_ready, zstats_ready, zmv_ready = (sem(s) for s in ("o_ps", "z_ready", "zstats_ready", "zmv_ready"))
    zstd_ready, zrstd_ready, zshift_ready, res_ready = (sem(s) for s in ("zstd_ready", "zrstd_ready", "zshift_ready", "res_ready"))

    def ge(eng, s, value):
        if isinstance(value, int) and value <= 0:
            return
        eng.wait_ge(s, value)

    def every_other(j, par):
        return 16 * (j // 2 + 1) if isinstance(j, int) else j * 8 + (16 - 8 * par)

    def stages(eng, n, last, head, body, ahead=0):
        for i in range(head):
            body(i, i % 2)
        stop = n - ahead - (n - ahead - head) % 2
        with eng.Fori(head, stop - 1, 2) as i:
            body(i, head % 2)
            body(i + 1, (head + 1) % 2)
        for i in range(stop, n + last):
            body(i, i % 2)

    def valid(j, n=NK):
        return not isinstance(j, int) or 0 <= j < n

    def halves(view, w0, nw, s):
        return [view[:, bass.ds(w0, nw), s, h * HB:(h + 1) * HB] for h in range(2)]

    def windows(t, p):
        n = T // p
        return t[:, 0:n * p, :].rearrange("f (w s) b -> f w s b", s=p)

    def flat(t, nw):
        return t[:, :, 0:nw * HB]

    def lstm_loop(eng, step):
        for n in range(2):
            step(n, STEPS[n], n % 2)
        with eng.Fori(2, N1 - 1, 2) as n:
            for m in range(2):
                step(n + m, STEPS[2 + m], m, w0=(n + m) * JW[1][0])
        with eng.Fori(0, N2 // 2) as q:
            for m in range(4):
                st = STEPS[N1 + m]
                at = dict(st, full=q * 2 + st["full"], need_x=q * 4 + st["need_x"], need_h=q * 4 + st["need_h"])
                step(q * 4 + (N1 + m), at, m % 2, w0=q * (2 * JW[2][0]) + st["w0"])
        for n in range(N1 + 2 * N2, NS):
            step(n, STEPS[n], n % 2)

    def cell_slot(st, par):
        return par if st["p"] == 1 else st["slot"]

    GRAPH_KEYS = 5 + ET * 4
    GRAPH_ROWS = GRAPH_KEYS + 3
    GRAPH_NODES = GRAPH_ROWS + JT
    GRAPH_DVE = GRAPH_NODES + 2 * JT + 2 * ET + 5 + 2 * ET + 1
    SOFT_SCORE = ET
    SOFT_SHIFTED = SOFT_SCORE + 5
    SOFT_WEIGHT = SOFT_SHIFTED + 5
    SOFT_ATTN = SOFT_WEIGHT + ET

    block = stacks["all"].enter_context(nc.Block())

    @block.sync
    def _(sp):
        sp.dma_start(adjT_raw[:, :, :], adjT).then_inc(first_in, 16)

        def load_x(j, par, loads_before, used, used_count):
            ge(sp, used, used_count)
            sp.dma_start(xs[par][:, :, :, :], x[bass.ds(j, 1)].rearrange("k p b j d -> p (k b) j d")
                         ).then_inc(x_in[par], 16)

        load_x(0, 0, 0, x_split, 0)
        sp.dma_start(wg_raw[:, 0, :], Wg0).then_inc(first_in, 16)
        sp.dma_start(wg_raw[:, 1, :], Wg1).then_inc(first_in, 16)
        load_x(1, 1, 0, x_split, 0)
        sp.wait_ge(zeroed, 1)
        for r in (0, 32, 64):
            sp.dma_start(b_raw[r:r + 1, 0, :], bg0).then_inc(row_in, 16)
        for r in (0, 32):
            sp.dma_start(b_raw[r:r + 1, 1, :], bg1).then_inc(row_in, 16)
        for h in range(NH):
            sp.dma_start(head_raw[h * DH:(h + 1) * DH, h:h + 1], a[h:h + 1, :].rearrange("o d -> d o")).then_inc(row_in, 16)
        with sp.Fori(2, NK - 1, 2) as j:
            load_x(j, 0, 0, x_split, j - 1)
            load_x(j + 1, 1, 0, x_split, j)
        load_x(0, 0, 0, x_split, NK)
        load_x(1, 1, 0, x_split, NK)
        with sp.Fori(2, NK - 1, 2) as j:
            load_x(j, 0, 0, y_ready, j - 1)
            load_x(j + 1, 1, 0, y_ready, j)

        def store(j, par):
            sp.wait_ge(res_ready, j + 1)
            sp.dma_start(out[bass.ds(j, 1)].rearrange("k p g d -> p (k g) d"), res[par][:, :, :]).then_inc(out_done[par], 16)

        with sp.Fori(0, NK - 1, 2) as j:
            store(j, 0)
            store(j + 1, 1)
        for par in range(2):
            sp.wait_ge(out_done[par], 16 * NK // 2)

    @block.gpsimd
    def _(pool):
        nc.gpsimd.memset(ident[:, :], 0.0).then_inc(iotas, 1)
        nc.gpsimd.iota(iota_i[:, :], pattern=[[1, T]], base=0, channel_multiplier=0).then_inc(iotas, 1)
        nc.gpsimd.iota(iota_ci[:, :], pattern=[[P, JT]], base=0, channel_multiplier=1).then_inc(iotas, 1)
        pool.wait_ge(iotas, 3)
        nc.gpsimd.affine_select(out=ident[:, :], in_=ident[:, :], compare_op=ALU.not_equal, fill=1.0,
                                base=0, pattern=[[-1, P]], channel_multiplier=1).then_inc(consts, 1)

        WC = 2 * SK * G4 // NK
        raw = wl_raw[:, :, :, :].rearrange("p a k g -> p (a k g)")
        whi = wl_hi[:, :, :, :].rearrange("p a k g -> p (a k g)")
        wlo = wl_lo[:, :, :, :].rearrange("p a k g -> p (a k g)")

        def first(i, par):
            pool.wait_ge(x_high, i + 1)
            nc.gpsimd.tensor_tensor(x_lo[par][:, :, :, :], xs[par][:, :, :, :], x_hi[par][:, :, :, :].bitcast(F32),
                                    ALU.subtract).then_inc(x_split, 1)
            pool.wait_ge(wl_in, 16 * 4)
            c = bass.ds(i * WC, WC)
            nc.gpsimd.tensor_copy(whi[:, c], raw[:, c]).then_inc(wl_high, 1)
            pool.wait_ge(wl_high, i + 1)
            nc.gpsimd.tensor_tensor(wlo[:, c], raw[:, c], whi[:, c].bitcast(F32), ALU.subtract).then_inc(wl_split, 1)

        with pool.Fori(0, NK - 1, 2) as i:
            first(i, 0)
            first(i + 1, 1)

        def h_low(n, st, par, w0=None):
            p, s, nw, slot = st["p"], st["s"], st["nw"], st["slot"]
            w0 = st["w0"] if w0 is None else w0
            pool.wait_ge(h_high, n + 1)
            o = flat(gate[GATE_O][par], nw)
            if s < p - 1:
                last = nc.gpsimd.tensor_tensor(flat(h_rec_lo[slot], nw), o, flat(h_rec_hi[slot], nw).bitcast(F32), ALU.subtract)
            else:
                his, los = halves(windows(hT_hi, p), w0, nw, s), halves(windows(hT_lo, p), w0, nw, s)
                for h in range(2):
                    last = nc.gpsimd.tensor_tensor(los[h], o[:, h, :].rearrange("f (w b) -> f w b", b=HB),
                                                   his[h].bitcast(F32), ALU.subtract)
            last.then_inc(h_split, 1)

        lstm_loop(pool, h_low)

        def hsum_make(j, par):
            ge(pool, t_ps, j - 1)
            hi = hT_hi[:, :, bass.ds(j * 2, 2)].rearrange("f t b -> f b t").bitcast(F32)
            lo = hT_lo[:, :, bass.ds(j * 2, 2)].rearrange("f t b -> f b t").bitcast(F32)
            nc.gpsimd.tensor_tensor(hsum[par][:, :, :], hi, lo, ALU.add).then_inc(hs_ready, 1)

        def graph(i, par):
            if valid(i - 4):
                pool.wait_ge(lr_high, i - 3)
                nc.gpsimd.tensor_tensor(lr_lo[par][:, :, :], lr[par][:, :, :],
                                        lr_hi[par][:, :, :].bitcast(F32), ALU.subtract).then_inc(lr_split, 1)
            if valid(i + 1):
                hsum_make(i + 1, 1 - par)
            if valid(i - 1):
                pool.wait_ge(x1_high, i)
                nc.gpsimd.tensor_tensor(x1_lo[1 - par][:, :, :], x1[:, bass.ds(i - 1, 1)].rearrange("p k g d -> p (k g) d"),
                                        x1_hi[1 - par][:, :, :].bitcast(F32), ALU.subtract).then_inc(x1_split, 1)

        pool.wait_ge(h_split, NS)
        hsum_make(0, 0)
        stages(pool, NK, 4, 6, graph, ahead=1)

        def rows(j, par):
            pool.wait_ge(vs_high, j + 1)
            nc.gpsimd.tensor_tensor(vs_lo[par][:, :, :], vs[par][:, :, :], vs_hi[par][:, :, :].bitcast(F32),
                                    ALU.subtract).then_inc(vs_split, 1)

        with pool.Fori(0, NK - 1, 2) as j:
            rows(j, 0)
            rows(j + 1, 1)

    @block.scalar
    def _(act):
        for i, w in enumerate((WihT, WhhT)):
            for k in range(0, SK, 2):
                act.dma_start(wl_raw[:, i, k:k + 2, :], w[:, k:k + 2, :]).then_inc(wl_in, 16)
        for i, w in enumerate((WlinT, WvalT, WoutT)):
            act.dma_start(lin_raw[:, i, :], w).then_inc(small_in, 16)
        act.dma_start(bias_ih[:, :, :], bih).then_inc(small_in, 16)
        act.dma_start(bias_hh[:, :, :], bhh).then_inc(small_in, 16)
        act.dma_start(adj_raw[:, :, :], adj).then_inc(small_in, 16)
        act.dma_start(ends_i[:, :], src.broadcast_to([P, E])).then_inc(ends_in, 16)
        act.dma_start(ends_ci[:, :, :], ends).then_inc(ends_in, 16)

        act.wait_ge(first_in, 48)
        nc.scalar.copy(adjT_hi[:, :, :], adjT_raw[:, :, :]).then_inc(act_prep, 1)
        for i in range(2):
            nc.scalar.copy(wg_hi[i][:, :], wg_raw[:, i, :]).then_inc(act_prep, 1)
        act.wait_ge(pe_prep, 1)
        for b in range(2):
            nc.scalar.copy(degree[:, b, :], ps_h2[0][:, 0:T]).then_inc(act_prep, 1)

        def first(i, par):
            if valid(i):
                act.wait_ge(x_in[par], every_other(i, par))
                ge(act, z_ps, i - 1)
                nc.scalar.copy(x_hi[par][:, :, :, :], xs[par][:, :, :, :]).then_inc(x_high, 1)
            if valid(i - 1):
                act.wait_ge(z_ps, i)
                nc.scalar.copy(z_hi[1 - par][:, :], ps_z[1 - par]).then_inc(z_high, 1)
            if valid(i - 2):
                act.wait_ge(h1_ps, i - 1)
                nc.scalar.activation(h1_hi[par][:, :], ps_h1[par], ACT.Relu).then_inc(h1_high, 1)
            if valid(i - 3):
                act.wait_ge(u_ps, i - 2)
                nc.scalar.copy(u_hi[1 - par][:, :, :, :].rearrange("p b j d -> p (b j d)"), ps_u[1 - par]).then_inc(u_high, 1)
            if valid(i - 4):
                act.wait_ge(h2_ps, i - 3)
                nc.scalar.activation(hT_hi[:, :, bass.ds((i - 4) * 2, 2)].rearrange("f t b -> f b t"),
                                     ps_h2[par].rearrange("f (b t) -> f b t", b=2), ACT.Relu).then_inc(h2_high, 1)

        stages(act, NK, 4, 6, first)

        def gates(n, st, par, w0=None):
            p, s, nw, slot, f = st["p"], st["s"], st["nw"], st["slot"], st["full"]
            for g in range(4):
                if g == GATE_F and s == 0:
                    continue
                act.wait_ge(gate_ps[g], (f if g == GATE_F else n) + 1)
                ge(act, h_split if g == GATE_O else c_ready, n - 1)
                r = GATE_ROW[g]
                nc.scalar.activation(flat(gate[g][par], nw), ps[:, 2 * g:2 * g + 2, 0:nw * HB], GATE_FUNC[g],
                                     bias=bias_gate[:, p - 1, r:r + 1]).then_inc(gate_sb[g], 1)
            act.wait_ge(c_ready, n + 1)
            nc.scalar.activation(flat(tanh_c[par], nw), flat(cell[cell_slot(st, par)], nw), ACT.Tanh).then_inc(tanh_ready, 1)

        lstm_loop(act, gates)

        def graph(i, par):
            if valid(i - 4):
                act.wait_ge(lr_ready, i - 3)
                ge(act, s_ps, i - 5)
                nc.scalar.copy(lr_hi[par][:, :, :], lr[par][:, :, :]).then_inc(lr_high, 1)
            if valid(i):
                act.wait_ge(mv_ready, i + 1)
                nc.scalar.activation(std[par][:, :], mv[par][:, :, 1], ACT.Sqrt, bias=eps_ln[:, :]).then_inc(std_ready, 1)
            if valid(i - 1):
                act.wait_ge(x1_ready, i)
                ge(act, gv_ps, i - 2)
                nc.scalar.copy(x1_hi[1 - par][:, :, :], x1[:, bass.ds(i - 1, 1)].rearrange("p k g d -> p (k g) d")).then_inc(x1_high, 1)
            if valid(i - 2):
                act.wait_ge(gv_ps, i - 1)
                ge(act, v_ps, i - 3)
                nc.scalar.copy(gv_hi[par][:, :, :, :].rearrange("p b g e -> p b (g e)"), ps_gv).then_inc(gv_high, 1)
            if valid(i - 3):
                act.wait_ge(q_ps, i - 2)
                ge(act, lr_ready, i - 4)
                nc.scalar.copy(qs[1 - par][:, :, :].rearrange("p b e -> p (b e)"), ps_q[1 - par]).then_inc(q_ready, 1)
                act.wait_ge(v_ps, i - 2)
                nc.scalar.copy(values[:, bass.ds(i - 3, 1)].rearrange("p k g d -> p (k g d)"), ps_v).then_inc(v_ready, 1)

        stages(act, NK, 4, 6, graph)

        act.wait_ge(graph_dve, GRAPH_DVE)
        nc.scalar.activation(log_adj[:, :], adj_edge[:, :], ACT.Ln).then_inc(soft_act, 1)
        act.wait_ge(soft_dve, SOFT_SHIFTED)
        nc.scalar.activation(ex[:, :], top[:, :], ACT.Exp).then_inc(soft_act, 1)

        def rows(i, par):
            if valid(i):
                act.wait_ge(vs_ready, i + 1)
                ge(act, yt_ps, i - 1)
                nc.scalar.copy(vs_hi[par][:, :, :], vs[par][:, :, :]).then_inc(vs_high, 1)
            if valid(i - 1):
                act.wait_ge(yt_ps, i)
                ge(act, o_ps, i - 2)
                nc.scalar.copy(yt_hi[1 - par][:, :, :].rearrange("p b t -> p (b t)"), ps_y[1 - par]).then_inc(yt_high, 1)
            if valid(i - 2):
                act.wait_ge(zmv_ready, i - 1)
                nc.scalar.activation(std[par][:, :], mv[par][:, :, 1], ACT.Sqrt, bias=eps_ln[:, :]).then_inc(zstd_ready, 1)
            if valid(i - 3):
                act.wait_ge(zshift_ready, i - 2)
                if not isinstance(i, int) or i - 3 >= 2:
                    act.wait_ge(out_done[1 - par], every_other(i - 5, 1 - par))
                for g in range(2 * JT):
                    last = nc.scalar.activation(res[1 - par][:, g, :], z[1 - par][:, g, :], ACT.Identity,
                                                bias=shift[1 - par][:, g:g + 1], scale=rstd[1 - par][:, g:g + 1])
                last.then_inc(res_ready, 1)

        stages(act, NK, 3, 6, rows)

    @block.vector
    def _(dve):
        nc.vector.memset(b_raw[:, :, :], 0.0).then_inc(dve_prep, 1)
        nc.vector.memset(head_raw[:, :], 0.0).then_inc(dve_prep, 1)
        dve.wait_ge(dve_prep, 2)
        nc.vector.memset(ones[:, :].bitcast(F32), 1.0).then_inc(zeroed, 1)
        nc.vector.memset(eps_ln[:, :], EPS_LN).then_inc(dve_prep, 1)
        dve.wait_ge(act_prep, 3)
        nc.vector.tensor_tensor(adjT_lo[:, :, :], adjT_raw[:, :, :], adjT_hi[:, :, :].bitcast(F32), ALU.subtract).then_inc(dve_prep, 1)
        for i in range(2):
            nc.vector.tensor_tensor(wg_lo[i][:, :], wg_raw[:, i, :], wg_hi[i][:, :].bitcast(F32), ALU.subtract).then_inc(dve_prep, 1)
        dve.wait_ge(row_in, 16 * (5 + NH))
        nc.vector.tensor_copy(bias0[:, :], b_raw[:, 0, :]).then_inc(dve_prep, 1)
        nc.vector.tensor_copy(bias1[:, :], b_raw[:, 1, :]).then_inc(dve_prep, 1)
        dve.wait_ge(dve_prep, 8)
        nc.vector.tensor_tensor(bias0[64:65, :], b_raw[64:65, 0, :], bias0[64:65, :].bitcast(F32), ALU.subtract).then_inc(dve_prep, 1)
        nc.vector.tensor_tensor(bias1[32:33, :], b_raw[32:33, 1, :], bias1[32:33, :].bitcast(F32), ALU.subtract).then_inc(dve_prep, 1)
        dve.wait_ge(act_prep, 5)
        for b in range(2):
            nc.vector.tensor_tensor(degree[32:64, b, :], ps_h2[0][32:64, 0:T], degree[32:64, b, :].bitcast(F32),
                                    ALU.subtract).then_inc(dve_prep, 1)

        def first(i, par):
            if valid(i - 1):
                dve.wait_ge(z_high, i)
                nc.vector.tensor_tensor(z_lo[1 - par][:, :], ps_z[1 - par], z_hi[1 - par][:, :].bitcast(F32),
                                        ALU.subtract).then_inc(z_split, 1)
            if valid(i - 2):
                dve.wait_ge(h1_high, i - 1)
                nc.vector.scalar_tensor_tensor(out=h1_lo[par][:, :], in0=ps_h1[par], scalar=0.0, in1=h1_hi[par][:, :].bitcast(F32),
                                               op0=ALU.max, op1=ALU.subtract).then_inc(h1_split, 1)
            if valid(i - 3):
                dve.wait_ge(u_high, i - 2)
                nc.vector.tensor_tensor(u_lo[1 - par][:, :, :, :].rearrange("p b j d -> p (b j d)"), ps_u[1 - par],
                                        u_hi[1 - par][:, :, :, :].rearrange("p b j d -> p (b j d)").bitcast(F32),
                                        ALU.subtract).then_inc(u_split, 1)
            if valid(i - 4):
                dve.wait_ge(h2_high, i - 3)
                b2 = bass.ds((i - 4) * 2, 2)
                nc.vector.scalar_tensor_tensor(out=hT_lo[:, :, b2].rearrange("f t b -> f b t"),
                                               in0=ps_h2[par].rearrange("f (b t) -> f b t", b=2), scalar=0.0,
                                               in1=hT_hi[:, :, b2].rearrange("f t b -> f b t").bitcast(F32),
                                               op0=ALU.max, op1=ALU.subtract).then_inc(h2_split, 1)

        stages(dve, NK, 4, 6, first)

        count = [0]

        def link(ins):
            count[0] += 1
            ins.then_inc(graph_dve, 1)
            dve.wait_ge(graph_dve, count[0])

        dve.wait_ge(iotas, 3)
        dve.wait_ge(ends_in, 32)
        dve.wait_ge(small_in, 16 * 6)
        link(nc.vector.tensor_copy(iota_row[:, :], iota_i[:, :]))
        link(nc.vector.tensor_copy(iota_col[:, :], iota_ci[:, :]))
        link(nc.vector.tensor_copy(ends_c[:, :, :], ends_ci[:, :, :]))
        link(nc.vector.tensor_scalar(key_row[:, :], ends_i[:, :], float(E), None, ALU.mult))
        link(nc.vector.tensor_tensor(key_row[:, :], key_row[:, :], iota_row[:, :], ALU.add))
        for j in range(ET):
            link(nc.vector.scalar_tensor_tensor(out=key_col[:, j:j + 1], in0=ends_c[:, j, 0:1], scalar=float(E),
                                                in1=iota_col[:, j:j + 1], op0=ALU.mult, op1=ALU.add))
            link(nc.vector.tensor_scalar(less[:, :], key_row[:, :], key_col[:, j:j + 1], None, ALU.is_lt))
            link(nc.vector.reduce_sum(rank[:, j:j + 1], less[:, :], AX_X))
            nc.vector.tensor_copy(ends_b[:, j, :, :], ends_c[:, j, :].unsqueeze(2).to_broadcast([P, 2, P]))
            link(nc.vector.tensor_scalar(order[:, j, :], iota_row[:, :], rank[:, j:j + 1], None, ALU.is_equal))
        assert count[0] == GRAPH_KEYS
        dve.wait_ge(graph_pe, 1)
        link(nc.vector.tensor_copy(ends_row[:, :, :], ps[:, 0:2, 0:E]))
        link(nc.vector.tensor_copy(ends_sc[:, :, :].rearrange("p j c -> p (j c)"), ps[:, 2, 0:2 * ET]))
        link(nc.vector.memset(same[:, :], 0.0))
        assert count[0] == GRAPH_ROWS
        for j in range(JT):
            link(nc.vector.tensor_scalar(src_node[:, j, :], ends_row[:, 0, :], iota_col[:, j:j + 1], None, ALU.is_equal))
        assert count[0] == GRAPH_NODES
        for j in range(JT):
            link(nc.vector.tensor_scalar(gather[:, j, 1, :], ends_row[:, 1, :], iota_col[:, j:j + 1], None, ALU.is_equal))
            link(nc.vector.tensor_tensor(gather[:, j, 0, :], src_node[:, j, :], gather[:, j, 1, :].bitcast(F32), ALU.add))
        for j in range(ET):
            link(nc.vector.tensor_scalar(scatter[:, j, :], iota_row[:, :], ends_sc[:, j, 0:1], None, ALU.is_equal))
            link(nc.vector.tensor_scalar(dst_edge[:, j, :], iota_row[:, :], ends_sc[:, j, 1:2], None, ALU.is_equal))
        link(nc.vector.tensor_tensor(same[:, 1:E], ends_row[:, 0, 1:E], ends_row[:, 0, 0:E - 1], ALU.is_equal))
        link(nc.vector.tensor_scalar(pen[:, :], same[:, :], BIG, -BIG, ALU.mult, ALU.add))
        link(nc.vector.tensor_copy(lin_hi[:, :, :], lin_raw[:, :, :]))
        nc.vector.tensor_tensor(lin_lo[:, :, :], lin_raw[:, :, :], lin_hi[:, :, :].bitcast(F32), ALU.subtract)
        nc.vector.tensor_tensor(bias_gate[:, :, :], bias_ih[:, :, :], bias_hh[:, :, :], ALU.add)
        link(nc.vector.tensor_copy(head_hi[:, :], head_raw[:, :]))
        link(nc.vector.tensor_tensor(head_lo[:, :], head_raw[:, :], head_hi[:, :].bitcast(F32), ALU.subtract))
        dve.wait_ge(graph_pe, 2)
        for j in range(ET):
            link(nc.vector.tensor_tensor(less[:, :], ps[:, 3 + j, 0:T], dst_edge[:, j, :], ALU.mult))
            link(nc.vector.reduce_sum(adj_edge[:, j:j + 1], less[:, :], AX_X))
        link(nc.vector.tensor_scalar(adj_edge[:, :], adj_edge[:, :], EPS_LOG, None, ALU.add))
        assert count[0] == GRAPH_DVE

        def update(n, st, par, w0=None):
            p, s, nw, slot, f = st["p"], st["s"], st["nw"], st["slot"], st["full"]
            w0 = st["w0"] if w0 is None else w0
            gi, gg, gf, go = (flat(gate[g][par], nw) for g in range(4))
            c = flat(cell[cell_slot(st, par)], nw)
            dve.wait_ge(gate_sb[GATE_I], n + 1)
            dve.wait_ge(gate_sb[GATE_G], n + 1)
            if s == 0:
                nc.vector.tensor_tensor(c, gi, gg, ALU.mult).then_inc(c_ready, 1)
            else:
                nc.vector.tensor_tensor(gg, gi, gg, ALU.mult).then_inc(in_gate, 1)
                dve.wait_ge(gate_sb[GATE_F], f + 1)
                nc.vector.tensor_tensor(gf, gf, c, ALU.mult).then_inc(keep_gate, 1)
                dve.wait_ge(in_gate, f + 1)
                dve.wait_ge(keep_gate, f + 1)
                nc.vector.tensor_tensor(c, gg, gf, ALU.add).then_inc(c_ready, 1)
            dve.wait_ge(tanh_ready, n + 1)
            dve.wait_ge(gate_sb[GATE_O], n + 1)
            nc.vector.tensor_tensor(go, go, flat(tanh_c[par], nw), ALU.mult).then_inc(h_ready, 1)
            dve.wait_ge(h_ready, n + 1)
            if s < p - 1:
                last = nc.vector.tensor_copy(flat(h_rec_hi[slot], nw), go)
            else:
                for h, dst_h in enumerate(halves(windows(hT_hi, p), w0, nw, s)):
                    last = nc.vector.tensor_copy(dst_h, go[:, h, :].rearrange("f (w b) -> f w b", b=HB))
            last.then_inc(h_high, 1)

        lstm_loop(dve, update)

        def graph(i, par):
            if valid(i):
                dve.wait_ge(t_ps, i + 1)
                dve.wait_ge(x_in[par], every_other(i, par) + 16 * NK // 2)
                ge(dve, x1_ready, i - 1)
                nc.vector.tensor_tensor(y[par][:, :, :].rearrange("p g d -> p (g d)"), ps_t[par],
                                        xs[par][:, :, :, :].rearrange("p b j d -> p (b j d)"), ALU.add).then_inc(y_ready, 1)
                dve.wait_ge(y_ready, i + 1)
                for g in range(2 * JT):
                    last = nc.vector.bn_stats(stat[par][:, g, :], y[par][:, g, :])
                last.then_inc(stats_ready, 1)
                dve.wait_ge(stats_ready, i + 1)
            if valid(i - 1):
                dve.wait_ge(std_ready, i)
                nc.vector.reciprocal(rstd[1 - par][:, :], std[1 - par][:, :]).then_inc(rstd_ready, 1)
            if valid(i):
                for g in range(2 * JT):
                    last = nc.vector.bn_aggr(mv[par][:, g, :], stat[par][:, g, :])
                last.then_inc(mv_ready, 1)
            if valid(i - 1):
                dve.wait_ge(rstd_ready, i)
                dst_rows = x1[:, bass.ds(i - 1, 1)].rearrange("p k g d -> p (k g) d")
                for g in range(2 * JT):
                    last = nc.vector.tensor_scalar(dst_rows[:, g, :], y[1 - par][:, g, :], mv[1 - par][:, g, 0:1],
                                                   rstd[1 - par][:, g:g + 1], ALU.subtract, ALU.mult)
                last.then_inc(x1_ready, 1)
            if valid(i - 2):
                dve.wait_ge(gv_high, i - 1)
                nc.vector.tensor_tensor(gv_lo[par][:, :, :, :].rearrange("p b g e -> p b (g e)"), ps_gv,
                                        gv_hi[par][:, :, :, :].rearrange("p b g e -> p b (g e)").bitcast(F32),
                                        ALU.subtract).then_inc(gv_split, 1)
            if valid(i - 3):
                dve.wait_ge(q_ready, i - 2)
                ge(dve, lr_split, i - 4)
                nc.vector.scalar_tensor_tensor(out=lr[1 - par][:, :, :].rearrange("p b e -> p (b e)"), in0=ps_q[1 - par],
                                               scalar=SLOPE, in1=qs[1 - par][:, :, :].rearrange("p b e -> p (b e)"),
                                               op0=ALU.mult, op1=ALU.max).then_inc(lr_ready, 1)

        stages(dve, NK, 3, 6, graph)

        soft = [0]

        def chain(ins):
            soft[0] += 1
            ins.then_inc(soft_dve, 1)
            dve.wait_ge(soft_dve, soft[0])

        dve.wait_ge(s_ps, NK)
        dve.wait_ge(soft_act, 1)
        for j in range(ET):
            chain(nc.vector.tensor_scalar(score_e[:, j, :], ps_s[:, j * BH:(j + 1) * BH], log_adj[:, j:j + 1], None, ALU.add))
        assert soft[0] == SOFT_SCORE
        dve.wait_ge(soft_pe, 1)
        chain(nc.vector.tensor_copy(score[:, :], ps_t[0][:, 0:E]))
        chain(nc.vector.tensor_tensor_scan(run_f[:, :], pen[:, 0:E], score[:, :], -BIG, ALU.add, ALU.max))
        chain(nc.vector.tensor_tensor_scan(run_b[:, ::-1], pen[:, E:0:-1], score[:, ::-1], -BIG, ALU.add, ALU.max))
        chain(nc.vector.tensor_tensor(top[:, :], run_f[:, :], run_b[:, :], ALU.max))
        chain(nc.vector.tensor_tensor(top[:, :], score[:, :], top[:, :], ALU.subtract))
        assert soft[0] == SOFT_SHIFTED
        dve.wait_ge(soft_act, 2)
        chain(nc.vector.tensor_tensor_scan(run_f[:, :], same[:, 0:E], ex[:, :], 0.0, ALU.mult, ALU.add))
        chain(nc.vector.tensor_tensor_scan(run_b[:, ::-1], same[:, E:0:-1], ex[:, ::-1], 0.0, ALU.mult, ALU.add))
        nc.vector.tensor_tensor(run_b[:, :], run_b[:, :], ex[:, :], ALU.subtract).then_inc(soft_dve, 1)
        soft[0] += 1
        dve.wait_ge(soft_dve, soft[0])
        nc.vector.tensor_tensor(den[:, :], run_f[:, :], run_b[:, :], ALU.add).then_inc(zeroed, 1)
        dve.wait_ge(zeroed, 2)
        chain(nc.vector.reciprocal(rden[:, :], den[:, :]))
        chain(nc.vector.tensor_tensor(weight[:, :], ex[:, :], rden[:, :], ALU.mult))
        assert soft[0] == SOFT_WEIGHT
        dve.wait_ge(soft_pe, 2)
        for j in range(ET):
            chain(nc.vector.tensor_copy(attn[:, :, j, :], ps_t[1][:, j * BH:(j + 1) * BH].rearrange("p (b h) -> p b h", h=NH)))
        assert soft[0] == SOFT_ATTN

        attn_k = attn[:, :, :, :].rearrange("p (k b) j h -> p k (b j h)", b=2)

        def rows(i, par):
            if valid(i):
                ge(dve, vs_split, i - 1)
                nc.vector.tensor_tensor(vs[par][:, :, :].rearrange("p g (h d) -> p (g h) d", h=NH),
                                        values[:, bass.ds(i, 1)].rearrange("p k g (h d) -> p (k g h) d", h=NH),
                                        attn_k[:, bass.ds(i, 1), :].rearrange("p k g -> p (k g)").unsqueeze(2)
                                        .to_broadcast([P, 2 * ET * NH, DH]), ALU.mult).then_inc(vs_ready, 1)
            if valid(i - 1):
                dve.wait_ge(yt_high, i)
                nc.vector.tensor_tensor(yt_lo[1 - par][:, :, :].rearrange("p b t -> p (b t)"), ps_y[1 - par],
                                        yt_hi[1 - par][:, :, :].rearrange("p b t -> p (b t)").bitcast(F32),
                                        ALU.subtract).then_inc(yt_split, 1)
            if valid(i - 2):
                dve.wait_ge(o_ps, i - 1)
                ge(dve, res_ready, i - 3)
                nc.vector.tensor_tensor(z[par][:, :, :].rearrange("p g d -> p (g d)"), ps_o[par],
                                        x1[:, bass.ds(i - 2, 1)].rearrange("p k g d -> p (k g d)"), ALU.add).then_inc(z_ready, 1)
                dve.wait_ge(z_ready, i - 1)
                for g in range(2 * JT):
                    last = nc.vector.bn_stats(stat[par][:, g, :], z[par][:, g, :])
                last.then_inc(zstats_ready, 1)
                dve.wait_ge(zstats_ready, i - 1)
            if valid(i - 3):
                dve.wait_ge(zstd_ready, i - 2)
                nc.vector.reciprocal(rstd[1 - par][:, :], std[1 - par][:, :]).then_inc(zrstd_ready, 1)
            if valid(i - 2):
                for g in range(2 * JT):
                    last = nc.vector.bn_aggr(mv[par][:, g, :], stat[par][:, g, :])
                last.then_inc(zmv_ready, 1)
            if valid(i - 3):
                dve.wait_ge(zrstd_ready, i - 2)
                nc.vector.scalar_tensor_tensor(out=shift[1 - par][:, :], in0=mv[1 - par][:, :, 0], scalar=-1.0,
                                               in1=rstd[1 - par][:, :], op0=ALU.mult, op1=ALU.mult).then_inc(zshift_ready, 1)

        stages(dve, NK, 3, 6, rows)

    @block.tensor
    def _(pe):
        def mm(out_, lhsT, rhs, start, stop):
            return nc.tensor.matmul(out_, lhsT, rhs, start=start, stop=stop, skip_group_check=True)

        pe.wait_ge(zeroed, 1)
        pe.wait_ge(dve_prep, 6)
        terms = [(part, j) for part in (adjT_hi, adjT_lo) for j in range(JT)]
        for n, (part, j) in enumerate(terms):
            last = mm(ps_h2[0][:, 0:T], ones[:, :], part[:, j, :], n == 0, n == len(terms) - 1)
        last.then_inc(pe_prep, 1)

        def adj_product(acc, hi, lo):
            for b in range(2):
                n = 0
                for rows, part in ((hi, adjT_hi), (hi, adjT_lo), (lo, adjT_hi)):
                    for j in range(JT):
                        last = mm(acc[:, b * T:(b + 1) * T], rows[:, b, j, :], part[:, j, :], n == 0, n == 3 * JT - 1)
                        n += 1
            return last

        def first(i, par):
            if valid(i):
                pe.wait_ge(x_split, i + 1)
                ge(pe, z_split, i - 1)
                adj_product(ps_z[par], x_hi[par], x_lo[par]).then_inc(z_ps, 1)
            if valid(i - 1):
                pe.wait_ge(z_split, i)
                if isinstance(i, int) and i == 1:
                    pe.wait_ge(dve_prep, 12)
                ge(pe, h1_split, i - 2)
                acc = ps_h1[1 - par]
                mm(acc, wg_hi[0][:, :], z_hi[1 - par][:, :], True, False)
                mm(acc, wg_hi[0][:, :], z_lo[1 - par][:, :], False, False)
                mm(acc, wg_lo[0][:, :], z_hi[1 - par][:, :], False, False)
                mm(acc, bias0[:, :], degree[:, :, :].rearrange("p b t -> p (b t)"), False, True).then_inc(h1_ps, 1)
            if valid(i - 2):
                pe.wait_ge(h1_split, i - 1)
                ge(pe, u_split, i - 3)
                acc = ps_u[par]
                for g in range(4):
                    mm(acc[:, g * D:(g + 1) * D], ones[:, :], bias1[:, :], g == 0, False)
                for g in range(4):
                    c = slice(g * P, (g + 1) * P)
                    mm(acc[:, c], h1_hi[par][:, c], wg_hi[1][:, :], False, False)
                    mm(acc[:, c], h1_hi[par][:, c], wg_lo[1][:, :], False, False)
                    last = mm(acc[:, c], h1_lo[par][:, c], wg_hi[1][:, :], False, g == 3)
                last.then_inc(u_ps, 1)
            if valid(i - 3):
                pe.wait_ge(u_split, i - 2)
                ge(pe, h2_split, i - 4)
                adj_product(ps_h2[1 - par], u_hi[1 - par], u_lo[1 - par]).then_inc(h2_ps, 1)

        stages(pe, NK, 3, 6, first)

        for s in (z_split, h1_split, u_split, h2_split):
            pe.wait_ge(s, NK)
        pe.wait_ge(graph_dve, GRAPH_KEYS)
        for c in range(2):
            for j in range(ET):
                mm(ps[:, c, 0:E], ends_b[:, j, c, :], order[:, j, :], j == 0, j == ET - 1)
        for r in range(ET):
            for j in range(ET):
                last = mm(ps[:, 2, 2 * r:2 * r + 2], order[:, j, r * P:(r + 1) * P], ends_c[:, j, :], j == 0, j == ET - 1)
        last.then_inc(graph_pe, 1)
        pe.wait_ge(graph_dve, GRAPH_NODES)
        for r in range(ET):
            for j in range(JT):
                last = mm(ps[:, 3 + r, 0:T], src_node[:, j, r * P:(r + 1) * P], adj_raw[:, j, :], j == 0, j == JT - 1)
        last.then_inc(graph_pe, 1)
        pe.wait_ge(graph_dve, GRAPH_DVE)
        pe.wait_ge(wl_split, NK)

        def gates(n, st, par, w0=None):
            p, s, nw, slot, f = st["p"], st["s"], st["nw"], st["slot"], st["full"]
            w0 = st["w0"] if w0 is None else w0
            x_parts = {"hi": halves(windows(hT_hi, p), w0, nw, s), "lo": halves(windows(hT_lo, p), w0, nw, s)}
            h_parts = {"hi": [h_rec_hi[slot][:, h, 0:nw * HB] for h in range(2)],
                       "lo": [h_rec_lo[slot][:, h, 0:nw * HB] for h in range(2)]}
            ge(pe, h_split, st["need_x"])
            waited = False
            for g in range(4):
                if g == GATE_F and s == 0:
                    continue
                ge(pe, gate_sb[g], f if g == GATE_F else n)
                r = GATE_ROW[g]
                c = slice(r * D, (r + 1) * D)
                products = [(0, wl_hi, x_parts["hi"]), (0, wl_hi, x_parts["lo"]), (0, wl_lo, x_parts["hi"])]
                if s > 0:
                    products += [(1, wl_hi, h_parts["hi"]), (1, wl_hi, h_parts["lo"]), (1, wl_lo, h_parts["hi"])]
                for k, (kind, w, parts) in enumerate(products):
                    if kind == 1 and not waited:
                        pe.wait_ge(h_split, st["need_h"])
                        waited = True
                    for h in range(2):
                        last = mm(ps[:, 2 * g + h, 0:nw * HB], w[:, kind, p - 1, c], parts[h], k == 0, k == len(products) - 1)
                last.then_inc(gate_ps[g], 1)

        lstm_loop(pe, gates)

        def graph(i, par):
            if valid(i):
                pe.wait_ge(hs_ready, i + 1)
                if isinstance(i, int) and i == 0:
                    for g in range(4):
                        pe.wait_ge(gate_sb[g], STEPS[-1]["full"] + 1 if g == GATE_F else NS)
                ge(pe, y_ready, i - 1)
                for b in range(2):
                    for j in range(JT):
                        c = (b * JT + j) * P
                        last = nc.tensor.transpose(ps_t[par][:, c:c + P], hsum[par][:, b, j * P:(j + 1) * P], ident[:, :])
                last.then_inc(t_ps, 1)
            if valid(i - 2):
                pe.wait_ge(x1_split, i - 1)
                ge(pe, gv_split, i - 2)
                for b in range(2):
                    n = 0
                    for part in (x1_hi[par], x1_lo[par]):
                        for j in range(JT):
                            last = mm(ps_gv[:, b, :], part[:, b * JT + j, :], gather[:, j, :, :].rearrange("p g e -> p (g e)"),
                                      n == 0, n == 2 * JT - 1)
                            n += 1
                last.then_inc(gv_ps, 1)
            if valid(i - 3):
                pe.wait_ge(gv_split, i - 2)
                ge(pe, lr_ready, i - 4)
                hi, lo = gv_hi[1 - par], gv_lo[1 - par]
                acc = ps_q[1 - par]
                mm(acc, lin_hi[:, 0, :], hi[:, :, 0, :], True, False)
                mm(acc, lin_hi[:, 0, :], lo[:, :, 0, :], False, False)
                mm(acc, lin_lo[:, 0, :], hi[:, :, 0, :], False, True).then_inc(q_ps, 1)
                ge(pe, v_ready, i - 3)
                for b in range(2):
                    for j in range(ET):
                        v = ps_v[:, (b * ET + j) * D:(b * ET + j + 1) * D]
                        e = slice(j * P, (j + 1) * P)
                        mm(v, hi[:, b, 1, e], lin_hi[:, 1, :], True, False)
                        mm(v, hi[:, b, 1, e], lin_lo[:, 1, :], False, False)
                        last = mm(v, lo[:, b, 1, e], lin_hi[:, 1, :], False, True)
                last.then_inc(v_ps, 1)
            if valid(i - 4):
                pe.wait_ge(lr_split, i - 3)
                for b in range(2):
                    for j in range(ET):
                        acc = ps_s[:, bass.ds((i - 4) * (2 * NH) + (j * BH + b * NH), NH)]
                        e = slice(j * P, (j + 1) * P)
                        mm(acc, lr_hi[par][:, b, e], head_hi[:, :], True, False)
                        mm(acc, lr_hi[par][:, b, e], head_lo[:, :], False, False)
                        last = mm(acc, lr_lo[par][:, b, e], head_hi[:, :], False, True)
                last.then_inc(s_ps, 1)

        stages(pe, NK, 4, 6, graph)

        pe.wait_ge(soft_dve, SOFT_SCORE)
        pe.wait_ge(y_ready, NK)
        for j in range(ET):
            last = nc.tensor.transpose(ps_t[0][:, j * P:(j + 1) * P], score_e[:, j, :], ident[:, :])
        last.then_inc(soft_pe, 1)
        pe.wait_ge(soft_dve, SOFT_WEIGHT)
        for j in range(ET):
            last = nc.tensor.transpose(ps_t[1][:, j * P:(j + 1) * P], weight[:, j * P:(j + 1) * P], ident[:, :])
        last.then_inc(soft_pe, 1)

        def rows(i, par):
            if valid(i):
                pe.wait_ge(vs_split, i + 1)
                ge(pe, yt_split, i - 1)
                for b in range(2):
                    n = 0
                    for part in (vs_hi[par], vs_lo[par]):
                        for j in range(ET):
                            last = mm(ps_y[par][:, b * T:(b + 1) * T], part[:, b * ET + j, :], scatter[:, j, :], n == 0, n == 2 * ET - 1)
                            n += 1
                last.then_inc(yt_ps, 1)
            if valid(i - 1):
                pe.wait_ge(yt_split, i)
                ge(pe, z_ready, i - 2)
                for b in range(2):
                    for j in range(JT):
                        o = ps_o[1 - par][:, (b * JT + j) * D:(b * JT + j + 1) * D]
                        t = slice(j * P, (j + 1) * P)
                        mm(o, yt_hi[1 - par][:, b, t], lin_hi[:, 2, :], True, False)
                        mm(o, yt_hi[1 - par][:, b, t], lin_lo[:, 2, :], False, False)
                        last = mm(o, yt_lo[1 - par][:, b, t], lin_hi[:, 2, :], False, True)
                last.then_inc(o_ps, 1)

        stages(pe, NK, 1, 4, rows)

    stacks["all"].close()


def kernel(x, adj, L0_gnn_Wg0, L0_gnn_bg0, L0_gnn_Wg1, L0_gnn_bg1, L0_gnn_Wih, L0_gnn_Whh, L0_gnn_bih, L0_gnn_bhh,
           L1_gnn_W_lin, L1_gnn_W_val, L1_gnn_a, L1_gnn_W_out, L1_gnn_src, L1_gnn_dst):
    import numpy as np
    import concourse.bacc as bacc
    from concourse.bass_utils import run_bass_kernel_spmd

    def arr(v):
        return np.asarray(v)

    def gates_first(b):
        b = arr(b)
        return b.reshape(b.shape[0], 4, -1).transpose(2, 0, 1)

    x = arr(x)
    Bn, T, D = x.shape
    JT = T // P
    adj = arr(adj)
    laid = {
        "x": x.reshape(Bn // 2, 2, JT, P, D).transpose(0, 3, 1, 2, 4),
        "adjT": adj.T.reshape(JT, P, T).transpose(1, 0, 2),
        "adj": adj.reshape(JT, P, T).transpose(1, 0, 2),
        "Wg0": arr(L0_gnn_Wg0), "bg0": arr(L0_gnn_bg0)[None],
        "Wg1": arr(L0_gnn_Wg1), "bg1": arr(L0_gnn_bg1)[None],
        "WihT": arr(L0_gnn_Wih).transpose(2, 0, 1), "WhhT": arr(L0_gnn_Whh).transpose(2, 0, 1),
        "bih": gates_first(L0_gnn_bih), "bhh": gates_first(L0_gnn_bhh),
        "WlinT": arr(L1_gnn_W_lin).T, "WvalT": arr(L1_gnn_W_val).T, "a": arr(L1_gnn_a), "WoutT": arr(L1_gnn_W_out).T,
        "src": arr(L1_gnn_src)[None],
        "ends": np.stack([arr(L1_gnn_src), arr(L1_gnn_dst)], -1).reshape(-1, P, 2).transpose(1, 0, 2),
    }
    laid = {k: np.ascontiguousarray(v) for k, v in laid.items()}
    nc = bacc.Bacc("TRN2", target_bir_lowering=False, num_devices=1)
    aps = [nc.dram_tensor(f"in_{k}", v.shape, mybir.dt.from_np(v.dtype), kind="ExternalInput").ap() for k, v in laid.items()]
    out = nc.dram_tensor("out", (Bn // 2, P, 2 * JT, D), F32, kind="ExternalOutput").ap()
    build(nc, *aps, out)
    r = run_bass_kernel_spmd(nc, [{f"in_{k}": v for k, v in laid.items()}], core_ids=[0])
    got = r.results[0]["out"]
    return got.reshape(Bn // 2, P, 2, JT, D).transpose(0, 2, 3, 1, 4).reshape(Bn, T, D)
```

```python
from contextlib import ExitStack

import concourse.bass as bass
from concourse import mybir

F32 = mybir.dt.float32
F32R = mybir.dt.float32r
I32 = mybir.dt.int32
ALU = mybir.AluOpType
ACT = mybir.ActivationFunctionType
AX_X = mybir.AxisListType.X

P = 128
BIG = 1e30

GATE_I, GATE_G, GATE_F, GATE_O = range(4)
GATE_ROW = {GATE_I: 0, GATE_F: 1, GATE_G: 2, GATE_O: 3}
GATE_FUNC = {GATE_I: ACT.Sigmoid, GATE_G: ACT.Tanh, GATE_F: ACT.Sigmoid, GATE_O: ACT.Sigmoid}


def lstm_steps(T, skips, job_windows):
    steps = []
    for p in range(1, skips + 1):
        jobs, w = [], 0
        for n in job_windows[p]:
            jobs.append((w, n))
            w += n
        assert w == T // p
        group = {1: 1, 2: 2, 3: len(jobs), 4: len(jobs)}[p]
        for g0 in range(0, len(jobs), group):
            for s in range(p):
                for slot, (w0, nw) in enumerate(jobs[g0:g0 + group]):
                    steps.append(dict(p=p, s=s, w0=w0, nw=nw, slot=slot, group=group,
                                      t0=w0 * p, t1=(w0 + nw) * p))
    full = 0
    for n, st in enumerate(steps):
        st["full"] = full
        full += st["s"] > 0
        need = 0
        for m in range(n):
            o = steps[m]
            if o["s"] == o["p"] - 1 and o["p"] < st["p"] and o["t0"] < st["t1"] and st["t0"] < o["t1"]:
                need = m + 1
        st["need_x"] = need
        st["need_h"] = n - st["group"] + 1
    return steps


def build(nc, x, adjT, adj, layers, WihT, WhhT, bih, bhh, linear, heads, src, ends, out):
    NK = x.shape[0]
    B = 2 * NK
    JT = x.shape[3]
    T = JT * P
    D = x.shape[4]
    SK = WihT.shape[1]
    G4 = 4 * D
    E = src.shape[1]
    ET = E // P
    NH = heads.shape[1]
    DH = D // NH
    BH = B * NH
    assert (D, T, E, BH, SK) == (P, 2 * P, 2 * P, P, 4)
    PB = 2 * T
    HB = B // 2
    HPAD = 4 * NH
    SLOPE, EPS_LN, EPS_LOG = 0.2, 1e-5, 1e-8

    JW = {1: [32] * 8, 2: [32] * 4, 3: [28, 28, 29], 4: [32, 32]}
    STEPS = lstm_steps(T, SK, JW)
    NS = len(STEPS)
    N1 = len(JW[1])
    N2 = len(JW[2])

    stacks = {k: ExitStack() for k in ("all", "weights", "first", "lstm", "edges", "graph", "rows")}

    def sb(stack, name, shape, dt=F32):
        return stacks[stack].enter_context(nc.sbuf_tensor(name, shape, dt))

    xs = [sb("all", f"xs{i}", [P, 2, JT, D]) for i in range(2)]
    ones = sb("all", "ones", [P, P], F32R)
    lin_raw = sb("all", "lin_raw", [P, 3, D])
    lin_hi = sb("all", "lin_hi", [P, D], F32R)
    lin_lo = sb("all", "lin_lo", [P, D], F32R)
    head_raw = sb("all", "head_raw", [P, NH])
    head_pad = sb("all", "head_pad", [P, 2, HPAD + NH], F32R)
    bias_ih = sb("all", "bias_ih", [P, SK, 4])
    bias_hh = sb("all", "bias_hh", [P, SK, 4])
    bias_gate = sb("all", "bias_gate", [P, SK, 4])
    ident = sb("all", "ident", [P, P])
    iota_row = sb("all", "iota_row", [P, T])
    iota_col = sb("all", "iota_col", [P, JT])
    gather = sb("all", "gather", [P, JT, 2, E], F32R)
    scatter = sb("all", "scatter", [P, ET, T])
    same = sb("all", "same", [P, E + 1])
    pen = sb("all", "pen", [P, E + 1])
    adj_edge = sb("all", "adj_edge", [P, ET])
    log_adj = sb("all", "log_adj", [P, ET])
    eps_ln = sb("all", "eps_ln", [P, 1])
    hT_hi = sb("all", "hT_hi", [P, T, B], F32R)
    hT_lo = sb("all", "hT_lo", [P, T, B], F32R)

    adj_raw = sb("weights", "adj_raw", [P, JT, T])
    ends_c = sb("weights", "ends_c", [P, ET, 2])
    ends_b = sb("weights", "ends_b", [P, ET, 2, P], F32R)
    order = sb("weights", "order", [P, ET, E], F32R)
    ends_row = sb("weights", "ends_row", [P, 2, E])
    ends_sc = sb("weights", "ends_sc", [P, ET, 2])
    src_node = sb("weights", "src_node", [P, JT, E])
    dst_edge = sb("weights", "dst_edge", [P, ET, T])
    picked = sb("weights", "picked", [P, T])
    wl_hi = sb("weights", "wl_hi", [P, 2, SK, G4], F32R)
    wl_lo = sb("weights", "wl_lo", [P, 2, SK, G4], F32R)

    adjT_hi = sb("first", "adjT_hi", [P, JT, T], F32R)
    adjT_lo = sb("first", "adjT_lo", [P, JT, T], F32R)
    wg_hi = sb("first", "wg_hi", [P, D], F32R)
    wg_lo = sb("first", "wg_lo", [P, D], F32R)
    bias0 = sb("first", "bias0", [P, D], F32R)
    bias1 = sb("first", "bias1", [P, D], F32R)
    degree = sb("first", "degree", [P, 2, T], F32R)
    adjT_raw = sb("first", "adjT_raw", [P, JT, T])
    layers_raw = sb("first", "layers_raw", [P, 4, D])
    wl_raw = sb("first", "wl_raw", [P, 2, SK, G4])
    x_hi = [sb("first", f"x_hi{i}", [P, 2, JT, D], F32R) for i in range(2)]
    x_lo = [sb("first", f"x_lo{i}", [P, 2, JT, D], F32R) for i in range(2)]
    z_hi = [sb("first", f"z_hi{i}", [P, PB], F32R) for i in range(2)]
    z_lo = [sb("first", f"z_lo{i}", [P, PB], F32R) for i in range(2)]
    h1 = [sb("first", f"h1_{i}", [P, PB]) for i in range(2)]
    u_hi = [sb("first", f"u_hi{i}", [P, 2, JT, D], F32R) for i in range(2)]
    u_lo = [sb("first", f"u_lo{i}", [P, 2, JT, D], F32R) for i in range(2)]
    iota_i = sb("first", "iota_i", [P, T], I32)
    iota_ci = sb("first", "iota_ci", [P, JT], I32)
    ends_i = sb("first", "ends_i", [P, E], I32)
    ends_ci = sb("first", "ends_ci", [P, ET, 2], I32)
    key_row = sb("first", "key_row", [P, E])
    key_col = sb("first", "key_col", [P, ET])
    less = sb("first", "less", [P, ET, E])
    rank = sb("first", "rank", [P, ET])
    stacks["first"].close()

    h_rec_hi = [sb("lstm", f"h_rec_hi{i}", [P, 2, 512], F32R) for i in range(3)]
    h_rec_lo = [sb("lstm", f"h_rec_lo{i}", [P, 2, 512], F32R) for i in range(3)]
    cell = [sb("lstm", f"cell{i}", [P, 2, 512]) for i in range(3)]
    gate = [[sb("lstm", f"gate{g}_{i}", [P, 2, 512]) for i in range(2)] for g in range(4)]
    tanh_c = [sb("lstm", f"tanh_c{i}", [P, 2, 512]) for i in range(2)]
    stacks["lstm"].close()
    stacks["weights"].close()

    values = sb("edges", "values", [P, NK, 2 * ET, D])
    x1 = sb("edges", "x1", [P, NK, 2 * JT, D])
    attn = sb("edges", "attn", [P, B, ET, NH])
    stat = [sb("edges", f"stat{i}", [P, 2 * JT, 6]) for i in range(2)]
    mv = [sb("edges", f"mv{i}", [P, 2 * JT, 2]) for i in range(2)]
    head_at = [sb("edges", f"head_at{i}", [P, 2, 2, HPAD + BH], F32R) for i in range(2)]
    log_diag = sb("edges", "log_diag", [P, ET, P])
    log_diag_hi = sb("edges", "log_diag_hi", [P, ET, P], F32R)
    log_diag_lo = sb("edges", "log_diag_lo", [P, ET, P], F32R)
    std = [sb("edges", f"std{i}", [P, 2 * JT]) for i in range(2)]
    rstd = [sb("edges", f"rstd{i}", [P, 2 * JT]) for i in range(2)]
    shift = [sb("edges", f"shift{i}", [P, 2 * JT]) for i in range(2)]

    hsum = [sb("graph", f"hsum{i}", [P, 2, T]) for i in range(2)]
    y = [sb("graph", f"y{i}", [P, 2 * JT, D]) for i in range(2)]
    x1_hi = [sb("graph", f"x1_hi{i}", [P, 2 * JT, D], F32R) for i in range(2)]
    x1_lo = [sb("graph", f"x1_lo{i}", [P, 2 * JT, D], F32R) for i in range(2)]
    both_hi = [sb("graph", f"both_hi{i}", [P, 2, E], F32R) for i in range(2)]
    both_lo = [sb("graph", f"both_lo{i}", [P, 2, E], F32R) for i in range(2)]
    dst_x = [sb("graph", f"dst_x{i}", [P, 2, E]) for i in range(2)]
    qs = [sb("graph", f"qs{i}", [P, 2, E]) for i in range(2)]
    lr = [sb("graph", f"lr{i}", [P, 2, E]) for i in range(2)]
    lr_hi = [sb("graph", f"lr_hi{i}", [P, 2, E], F32R) for i in range(2)]
    lr_lo = [sb("graph", f"lr_lo{i}", [P, 2, E], F32R) for i in range(2)]
    stacks["graph"].close()

    run_f = sb("rows", "run_f", [P, E])
    run_b = sb("rows", "run_b", [P, E])
    top = sb("rows", "top", [P, E])
    ex = sb("rows", "ex", [P, E])
    den = sb("rows", "den", [P, E])
    rden = sb("rows", "rden", [P, E])
    weight = sb("rows", "weight", [P, E])
    vs = [sb("rows", f"vs{i}", [P, 2 * ET, D]) for i in range(2)]
    yt = [sb("rows", f"yt{i}", [P, 2, T]) for i in range(2)]
    res = [sb("rows", f"res{i}", [P, 2 * JT, D]) for i in range(2)]
    stacks["rows"].close()
    stacks["edges"].close()

    ps = stacks["all"].enter_context(nc.psum_tensor("ps", [P, 8, 512], F32))
    ps_z = [ps[:, i, :] for i in range(2)]
    ps_h1 = [ps[:, 2 + i, :] for i in range(2)]
    ps_u = [ps[:, 4 + i, :] for i in range(2)]
    ps_h2 = [ps[:, 6 + i, :] for i in range(2)]
    ps_gv = [ps[:, 2 * i:2 * i + 2, :] for i in range(2)]
    ps_t = ps[:, 4, :]
    ps_q = ps[:, 5, :]
    ps_v = ps[:, 6, :]
    ps_s = ps[:, 7, 0:E]
    ps_y = [ps[:, i, :] for i in range(2)]
    ps_o = [ps[:, 2 + i, :] for i in range(2)]

    def sem(name):
        return stacks["all"].enter_context(nc.semaphore(name))

    first_in, small_in, wl_in, ends_in = (sem(s) for s in ("first_in", "small_in", "wl_in", "ends_in"))
    x_in = [sem("x_in0"), sem("x_in1")]
    out_done = [sem("out_done0"), sem("out_done1")]
    consts, iotas, ones_ready = sem("consts"), sem("iotas"), sem("ones_ready")
    act_prep, dve_prep, pe_prep, pool_prep = (sem(s) for s in ("act_prep", "dve_prep", "pe_prep", "pool_prep"))
    x_high, x_split = sem("x_high"), sem("x_split")
    z_ps, z_high, z_split = sem("z_ps"), sem("z_high"), sem("z_split")
    h1_ps, h1_ready = sem("h1_ps"), sem("h1_ready")
    u_ps, u_high, u_split = sem("u_ps"), sem("u_high"), sem("u_split")
    h2_ps, h2_high, h2_split = sem("h2_ps"), sem("h2_high"), sem("h2_split")
    wl_high, wl_split = sem("wl_high"), sem("wl_split")
    head_ready, log_ready, bias_ready = sem("head_ready"), sem("log_ready"), sem("bias_ready")
    graph_dve, graph_pe = sem("graph_dve"), sem("graph_pe")
    gate_ps = [sem(f"gate_ps{g}") for g in range(4)]
    gate_sb = [sem(f"gate_sb{g}") for g in range(4)]
    in_gate, keep_gate, c_ready, tanh_ready = (sem(s) for s in ("in_gate", "keep_gate", "c_ready", "tanh_ready"))
    h_ready, h_high, h_split = sem("h_ready"), sem("h_high"), sem("h_split")
    hs_ready, t_ps, y_ready, stats_ready, mv_ready = (sem(s) for s in ("hs_ready", "t_ps", "y_ready", "stats_ready", "mv_ready"))
    std_ready, rstd_ready, x1_ready, x1_high, x1_split = (sem(s) for s in ("std_ready", "rstd_ready", "x1_ready", "x1_high", "x1_split"))
    gv_ps, both_high, dst_ready, both_split = (sem(s) for s in ("gv_ps", "both_high", "dst_ready", "both_split"))
    q_ps, q_ready, lr_ready, lr_high, lr_split = (sem(s) for s in ("q_ps", "q_ready", "lr_ready", "lr_high", "lr_split"))
    v_ps, v_ready, s_ps = sem("v_ps"), sem("v_ready"), sem("s_ps")
    soft_dve, soft_act, soft_pe = sem("soft_dve"), sem("soft_act"), sem("soft_pe")
    vs_ready = sem("vs_ready")
    yt_ps, yt_ready = sem("yt_ps"), sem("yt_ready")
    o_ps, z_ready, zstats_ready, zmv_ready = (sem(s) for s in ("o_ps", "z_ready", "zstats_ready", "zmv_ready"))
    zstd_ready, zrstd_ready, zshift_ready, res_ready = (sem(s) for s in ("zstd_ready", "zrstd_ready", "zshift_ready", "res_ready"))

    def ge(eng, s, value):
        if isinstance(value, int) and value <= 0:
            return
        eng.wait_ge(s, value)

    def every_other(j, par):
        return 16 * (j // 2 + 1) if isinstance(j, int) else j * 8 + (16 - 8 * par)

    def stages(eng, n, last, head, body, ahead=0):
        for i in range(head):
            body(i, i % 2)
        stop = n - ahead - (n - ahead - head) % 2
        with eng.Fori(head, stop - 1, 2) as i:
            body(i, head % 2)
            body(i + 1, (head + 1) % 2)
        for i in range(stop, n + last):
            body(i, i % 2)

    def valid(j, n=NK):
        return not isinstance(j, int) or 0 <= j < n

    def halves(view, w0, nw, s):
        return [view[:, bass.ds(w0, nw), s, h * HB:(h + 1) * HB] for h in range(2)]

    def windows(t, p):
        n = T // p
        return t[:, 0:n * p, :].rearrange("f (w s) b -> f w s b", s=p)

    def flat(t, nw):
        return t[:, :, 0:nw * HB]

    def lstm_loop(eng, step, before=None, after=None):
        for n in range(2):
            step(n, STEPS[n], n % 2)
        with eng.Fori(2, N1 - 1, 2) as n:
            for m in range(2):
                step(n + m, STEPS[2 + m], m, w0=(n + m) * JW[1][0])
        with eng.Fori(0, N2 // 2) as q:
            for m in range(4):
                st = STEPS[N1 + m]
                at = dict(st, full=q * 2 + st["full"], need_x=q * 4 + st["need_x"], need_h=q * 4 + st["need_h"])
                step(q * 4 + (N1 + m), at, m % 2, w0=q * (2 * JW[2][0]) + st["w0"])
        for n in range(N1 + 2 * N2, NS):
            if before is not None:
                before(n)
            step(n, STEPS[n], n % 2)
            if after is not None:
                after(n)

    def cell_slot(st, par):
        return par if st["p"] == 1 else st["slot"]

    KEYS = 5
    GRAPH_ORDER = 2 * ET
    GRAPH_NODES = GRAPH_ORDER + 3 + JT
    GRAPH_EDGES = GRAPH_NODES + 1
    GRAPH_DVE = GRAPH_EDGES + 2 * ET + 1
    SOFT_SHIFTED = 4
    SOFT_WEIGHT = SOFT_SHIFTED + 6
    SOFT_ATTN = SOFT_WEIGHT + ET
    ENDS_STEP = N1 + 2 * N2
    ROWS_STEP = ENDS_STEP + 2
    assert all(STEPS[n]["s"] == 0 for n in range(ENDS_STEP, ROWS_STEP + 1))

    block = stacks["all"].enter_context(nc.Block())

    @block.sync
    def _(sp):
        sp.dma_start(adjT_raw[:, :, :], adjT).then_inc(first_in, 16)

        def load_x(j, par, used, used_count):
            ge(sp, used, used_count)
            sp.dma_start(xs[par][:, :, :, :], x[bass.ds(j, 1)].rearrange("k p b j d -> p (k b) j d")
                         ).then_inc(x_in[par], 16)

        load_x(0, 0, x_split, 0)
        sp.dma_start(layers_raw[:, :, :], layers).then_inc(first_in, 16)
        load_x(1, 1, x_split, 0)
        for i, w in enumerate((WihT, WhhT)):
            sp.dma_start(wl_raw[:, i, :, :], w).then_inc(wl_in, 16)
        sp.dma_start(ends_i[:, :], src.broadcast_to([P, E])).then_inc(ends_in, 16)
        sp.dma_start(ends_ci[:, :, :], ends).then_inc(ends_in, 16)
        for t, d in ((bias_ih, bih), (bias_hh, bhh), (lin_raw, linear), (adj_raw, adj)):
            sp.dma_start(t[:, :, :], d).then_inc(small_in, 16)
        sp.dma_start(head_raw[:, :], heads).then_inc(small_in, 16)
        with sp.Fori(2, NK - 1, 2) as j:
            load_x(j, 0, x_split, j - 1)
            load_x(j + 1, 1, x_split, j)
        load_x(0, 0, x_split, NK)
        load_x(1, 1, x_split, NK)
        with sp.Fori(2, NK - 1, 2) as j:
            load_x(j, 0, y_ready, j - 1)
            load_x(j + 1, 1, y_ready, j)

        def store(j, par):
            sp.wait_ge(res_ready, j + 1)
            sp.dma_start(out[bass.ds(j, 1)].rearrange("k p g d -> p (k g) d"), res[par][:, :, :]).then_inc(out_done[par], 16)

        with sp.Fori(0, NK - 1, 2) as j:
            store(j, 0)
            store(j + 1, 1)
        for par in range(2):
            sp.wait_ge(out_done[par], 16 * NK // 2)

    @block.gpsimd
    def _(pool):
        nc.gpsimd.memset(ident[:, :], 0.0).then_inc(iotas, 1)
        nc.gpsimd.iota(iota_i[:, :], pattern=[[1, T]], base=0, channel_multiplier=0).then_inc(iotas, 1)
        nc.gpsimd.iota(iota_ci[:, :], pattern=[[P, JT]], base=0, channel_multiplier=1).then_inc(iotas, 1)
        pool.wait_ge(iotas, 3)
        nc.gpsimd.affine_select(out=ident[:, :], in_=ident[:, :], compare_op=ALU.not_equal, fill=1.0,
                                base=0, pattern=[[-1, P]], channel_multiplier=1).then_inc(consts, 1)

        WC = 2 * SK * G4 // NK
        raw = wl_raw[:, :, :, :].rearrange("p a k g -> p (a k g)")
        whi = wl_hi[:, :, :, :].rearrange("p a k g -> p (a k g)")
        wlo = wl_lo[:, :, :, :].rearrange("p a k g -> p (a k g)")

        def first(i, par):
            if valid(i):
                pool.wait_ge(x_high, i + 1)
                nc.gpsimd.tensor_tensor(x_lo[par][:, :, :, :], xs[par][:, :, :, :], x_hi[par][:, :, :, :].bitcast(F32),
                                        ALU.subtract).then_inc(x_split, 1)
            if valid(i - 2):
                pool.wait_ge(wl_in, 16 * 2)
                c = bass.ds((i - 2) * WC, WC)
                nc.gpsimd.tensor_copy(whi[:, c], raw[:, c]).then_inc(wl_high, 1)
                pool.wait_ge(wl_high, i - 1)
                nc.gpsimd.tensor_tensor(wlo[:, c], raw[:, c], whi[:, c].bitcast(F32), ALU.subtract).then_inc(wl_split, 1)

        stages(pool, NK, 2, 4, first)

        keys = [0]

        def link(ins):
            keys[0] += 1
            ins.then_inc(pool_prep, 1)
            pool.wait_ge(pool_prep, keys[0])

        pool.wait_ge(ends_in, 32)
        nc.gpsimd.tensor_copy(iota_row[:, :], iota_i[:, :])
        nc.gpsimd.tensor_copy(iota_col[:, :], iota_ci[:, :])
        nc.gpsimd.tensor_copy(ends_c[:, :, :], ends_ci[:, :, :])
        link(nc.gpsimd.tensor_scalar(key_row[:, :], ends_i[:, :], float(E), None, ALU.mult))
        link(nc.gpsimd.tensor_tensor(key_row[:, :], key_row[:, :], iota_row[:, :], ALU.add))
        link(nc.gpsimd.tensor_scalar(key_col[:, :], ends_c[:, :, 0], float(E), None, ALU.mult))
        link(nc.gpsimd.tensor_tensor(key_col[:, :], key_col[:, :], iota_col[:, :], ALU.add))
        for j in range(ET):
            nc.gpsimd.tensor_scalar(less[:, j, :], key_row[:, :], key_col[:, j:j + 1], None, ALU.is_lt)
            last = nc.gpsimd.tensor_copy(ends_b[:, j, :, :], ends_c[:, j, :].unsqueeze(2).to_broadcast([P, 2, P]))
        link(last)
        assert keys[0] == KEYS

        def h_low(n, st, par, w0=None):
            p, s, nw, slot = st["p"], st["s"], st["nw"], st["slot"]
            w0 = st["w0"] if w0 is None else w0
            pool.wait_ge(h_high, n + 1)
            o = flat(gate[GATE_O][par], nw)
            if s < p - 1:
                last = nc.gpsimd.tensor_tensor(flat(h_rec_lo[slot], nw), o, flat(h_rec_hi[slot], nw).bitcast(F32), ALU.subtract)
            else:
                his, los = halves(windows(hT_hi, p), w0, nw, s), halves(windows(hT_lo, p), w0, nw, s)
                for h in range(2):
                    last = nc.gpsimd.tensor_tensor(los[h], o[:, h, :].rearrange("f (w b) -> f w b", b=HB),
                                                   his[h].bitcast(F32), ALU.subtract)
            last.then_inc(h_split, 1)

        lstm_loop(pool, h_low)

        def hsum_make(j, par):
            ge(pool, t_ps, j - 1)
            hi = hT_hi[:, :, bass.ds(j * 2, 2)].rearrange("f t b -> f b t").bitcast(F32)
            lo = hT_lo[:, :, bass.ds(j * 2, 2)].rearrange("f t b -> f b t").bitcast(F32)
            nc.gpsimd.tensor_tensor(hsum[par][:, :, :], hi, lo, ALU.add).then_inc(hs_ready, 1)

        def graph(i, par):
            if valid(i + 2):
                hsum_make(i + 2, par)
            if valid(i - 2):
                pool.wait_ge(x1_high, i - 1)
                nc.gpsimd.tensor_tensor(x1_lo[par][:, :, :], x1[:, bass.ds(i - 2, 1)].rearrange("p k g d -> p (k g) d"),
                                        x1_hi[par][:, :, :].bitcast(F32), ALU.subtract).then_inc(x1_split, 1)
            if valid(i - 7):
                pool.wait_ge(lr_high, i - 6)
                nc.gpsimd.tensor_tensor(lr_lo[1 - par][:, :, :], lr[1 - par][:, :, :],
                                        lr_hi[1 - par][:, :, :].bitcast(F32), ALU.subtract).then_inc(lr_split, 1)

        pool.wait_ge(h_split, NS)
        hsum_make(0, 0)
        hsum_make(1, 1)
        stages(pool, NK, 7, 8, graph, ahead=2)

    @block.scalar
    def _(act):
        act.wait_ge(first_in, 32)
        nc.scalar.copy(adjT_hi[:, :, :], adjT_raw[:, :, :]).then_inc(act_prep, 1)
        nc.scalar.copy(wg_hi[:, :], layers_raw[:, 0, :]).then_inc(act_prep, 1)
        act.wait_ge(pe_prep, 1)
        for b in range(2):
            nc.scalar.copy(degree[:, b, :], ps_h2[0][:, 0:T]).then_inc(act_prep, 1)

        def first(i, par):
            if valid(i):
                act.wait_ge(x_in[par], every_other(i, par))
                ge(act, z_ps, i - 1)
                nc.scalar.copy(x_hi[par][:, :, :, :], xs[par][:, :, :, :]).then_inc(x_high, 1)
            if valid(i - 1):
                act.wait_ge(z_ps, i)
                nc.scalar.copy(z_hi[1 - par][:, :], ps_z[1 - par]).then_inc(z_high, 1)
            if valid(i - 2):
                act.wait_ge(h1_ps, i - 1)
                nc.scalar.activation(h1[par][:, :], ps_h1[par], ACT.Relu).then_inc(h1_ready, 1)
            if valid(i - 3):
                act.wait_ge(u_ps, i - 2)
                nc.scalar.copy(u_hi[1 - par][:, :, :, :].rearrange("p b j d -> p (b j d)"), ps_u[1 - par]).then_inc(u_high, 1)
            if valid(i - 4):
                act.wait_ge(h2_ps, i - 3)
                nc.scalar.activation(hT_hi[:, :, bass.ds((i - 4) * 2, 2)].rearrange("f t b -> f b t"),
                                     ps_h2[par].rearrange("f (b t) -> f b t", b=2), ACT.Relu).then_inc(h2_high, 1)

        stages(act, NK, 4, 6, first)

        def gates(n, st, par, w0=None):
            p, s, nw, slot, f = st["p"], st["s"], st["nw"], st["slot"], st["full"]
            for g in range(4):
                if g == GATE_F and s == 0:
                    continue
                act.wait_ge(gate_ps[g], (f if g == GATE_F else n) + 1)
                ge(act, h_split if g == GATE_O else c_ready, n - 1)
                r = GATE_ROW[g]
                nc.scalar.activation(flat(gate[g][par], nw), ps[:, 2 * g:2 * g + 2, 0:nw * HB], GATE_FUNC[g],
                                     bias=bias_gate[:, p - 1, r:r + 1]).then_inc(gate_sb[g], 1)
                if g == GATE_I:
                    flush()
            pending.append((n, st, par))
            if s > 0:
                flush()

        pending = []

        def flush():
            if pending:
                m, st, par = pending.pop()
                act.wait_ge(c_ready, m + 1)
                nc.scalar.activation(flat(tanh_c[par], st["nw"]), flat(cell[cell_slot(st, par)], st["nw"]),
                                     ACT.Tanh).then_inc(tanh_ready, 1)

        act.wait_ge(bias_ready, 1)
        for n in range(2):
            gates(n, STEPS[n], n % 2)
        with act.Fori(2, N1 - 1, 2) as n:
            pending[:] = [(n - 1, STEPS[1], 1)]
            for m in range(2):
                gates(n + m, STEPS[2 + m], m)
        pending[:] = [(N1 - 1, STEPS[N1 - 1], (N1 - 1) % 2)]
        flush()
        with act.Fori(0, N2 // 2) as q:
            for m in range(4):
                gates(q * 4 + (N1 + m), dict(STEPS[N1 + m], full=q * 2 + STEPS[N1 + m]["full"]), m % 2)
        for n in range(N1 + 2 * N2, NS):
            gates(n, STEPS[n], n % 2)

        act.wait_ge(graph_dve, GRAPH_DVE)
        nc.scalar.activation(log_adj[:, :], adj_edge[:, :], ACT.Ln).then_inc(log_ready, 1)

        def graph(i, par):
            if valid(i - 6):
                act.wait_ge(q_ps, i - 5)
                ge(act, lr_ready, i - 7)
                nc.scalar.copy(qs[par][:, :, :].rearrange("p b e -> p (b e)"), ps_q).then_inc(q_ready, 1)
                act.wait_ge(v_ps, i - 5)
                nc.scalar.copy(values[:, bass.ds(i - 6, 1)].rearrange("p k g d -> p (k g d)"), ps_v).then_inc(v_ready, 1)
            if valid(i - 2):
                act.wait_ge(x1_ready, i - 1)
                ge(act, gv_ps, i - 3)
                nc.scalar.copy(x1_hi[par][:, :, :], x1[:, bass.ds(i - 2, 1)].rearrange("p k g d -> p (k g) d")).then_inc(x1_high, 1)
            if valid(i - 4):
                act.wait_ge(gv_ps, i - 3)
                ge(act, v_ps, i - 5)
                nc.scalar.copy(dst_x[par][:, :, :], ps_gv[par][:, :, E:2 * E]).then_inc(dst_ready, 1)
                nc.scalar.copy(both_hi[par][:, :, :], ps_gv[par][:, :, 0:E]).then_inc(both_high, 1)
            if valid(i - 7):
                act.wait_ge(lr_ready, i - 6)
                ge(act, s_ps, i - 8)
                nc.scalar.copy(lr_hi[1 - par][:, :, :], lr[1 - par][:, :, :]).then_inc(lr_high, 1)
            if valid(i):
                act.wait_ge(mv_ready, i + 1)
                nc.scalar.activation(std[par][:, :], mv[par][:, :, 1], ACT.Sqrt, bias=eps_ln[:, :]).then_inc(std_ready, 1)

        stages(act, NK, 7, 10, graph)

        act.wait_ge(soft_dve, SOFT_SHIFTED)
        nc.scalar.activation(ex[:, :], top[:, :], ACT.Exp).then_inc(soft_act, 1)

        def rows(i, par):
            if valid(i - 2):
                act.wait_ge(yt_ps, i - 1)
                ge(act, o_ps, i - 3)
                nc.scalar.copy(yt[par][:, :, :].rearrange("p b t -> p (b t)"), ps_y[par]).then_inc(yt_ready, 1)
            if valid(i - 6):
                act.wait_ge(zshift_ready, i - 5)
                if not isinstance(i, int) or i - 6 >= 2:
                    act.wait_ge(out_done[par], every_other(i - 8, par))
                at = bass.ds(i - 6, 1)
                for g in range(2 * JT):
                    last = nc.scalar.activation(res[par][:, g, :], x1[:, at, g, :].rearrange("p k d -> p (k d)"), ACT.Identity,
                                                bias=shift[par][:, g:g + 1], scale=rstd[par][:, g:g + 1])
                last.then_inc(res_ready, 1)
            if valid(i - 4):
                act.wait_ge(zmv_ready, i - 3)
                nc.scalar.activation(std[par][:, :], mv[par][:, :, 1], ACT.Sqrt, bias=eps_ln[:, :]).then_inc(zstd_ready, 1)

        stages(act, NK, 6, 8, rows)

    @block.vector
    def _(dve):
        nc.vector.memset(ones[:, :].bitcast(F32), 1.0).then_inc(ones_ready, 1)
        nc.vector.memset(eps_ln[:, :], EPS_LN)
        dve.wait_ge(act_prep, 2)
        nc.vector.tensor_tensor(adjT_lo[:, :, :], adjT_raw[:, :, :], adjT_hi[:, :, :].bitcast(F32), ALU.subtract).then_inc(dve_prep, 1)
        nc.vector.tensor_tensor(wg_lo[:, :], layers_raw[:, 0, :], wg_hi[:, :].bitcast(F32), ALU.subtract).then_inc(dve_prep, 1)
        nc.vector.tensor_copy(bias0[:, :], layers_raw[:, 2, :]).then_inc(dve_prep, 1)
        nc.vector.tensor_copy(bias1[:, :], layers_raw[:, 3, :]).then_inc(dve_prep, 1)
        dve.wait_ge(dve_prep, 4)
        nc.vector.tensor_tensor(bias0[64:65, :], layers_raw[64:65, 2, :], bias0[64:65, :].bitcast(F32), ALU.subtract).then_inc(dve_prep, 1)
        nc.vector.tensor_tensor(bias1[32:33, :], layers_raw[32:33, 3, :], bias1[32:33, :].bitcast(F32), ALU.subtract).then_inc(dve_prep, 1)
        dve.wait_ge(act_prep, 4)
        for b in range(2):
            nc.vector.tensor_tensor(degree[32:64, b, :], ps_h2[0][32:64, 0:T], degree[32:64, b, :].bitcast(F32),
                                    ALU.subtract).then_inc(dve_prep, 1)

        def first(i, par):
            if valid(i - 1):
                dve.wait_ge(z_high, i)
                nc.vector.tensor_tensor(z_lo[1 - par][:, :], ps_z[1 - par], z_hi[1 - par][:, :].bitcast(F32),
                                        ALU.subtract).then_inc(z_split, 1)
            if valid(i - 3):
                dve.wait_ge(u_high, i - 2)
                nc.vector.tensor_tensor(u_lo[1 - par][:, :, :, :].rearrange("p b j d -> p (b j d)"), ps_u[1 - par],
                                        u_hi[1 - par][:, :, :, :].rearrange("p b j d -> p (b j d)").bitcast(F32),
                                        ALU.subtract).then_inc(u_split, 1)
            if valid(i - 4):
                dve.wait_ge(h2_high, i - 3)
                b2 = bass.ds((i - 4) * 2, 2)
                nc.vector.scalar_tensor_tensor(out=hT_lo[:, :, b2].rearrange("f t b -> f b t"),
                                               in0=ps_h2[par].rearrange("f (b t) -> f b t", b=2), scalar=0.0,
                                               in1=hT_hi[:, :, b2].rearrange("f t b -> f b t").bitcast(F32),
                                               op0=ALU.max, op1=ALU.subtract).then_inc(h2_split, 1)

        stages(dve, NK, 4, 6, first)

        count = [0]

        def link(ins):
            count[0] += 1
            ins.then_inc(graph_dve, 1)
            dve.wait_ge(graph_dve, count[0])

        dve.wait_ge(pool_prep, KEYS)
        for j in range(ET):
            link(nc.vector.reduce_sum(rank[:, j:j + 1], less[:, j, :], AX_X))
            link(nc.vector.tensor_scalar(order[:, j, :], iota_row[:, :], rank[:, j:j + 1], None, ALU.is_equal))
        assert count[0] == GRAPH_ORDER
        dve.wait_ge(small_in, 16 * 5)
        nc.vector.tensor_tensor(bias_gate[:, :, :], bias_ih[:, :, :], bias_hh[:, :, :], ALU.add).then_inc(bias_ready, 1)

        def set_up_first(n):
            if n == ENDS_STEP:
                dve.wait_ge(graph_pe, 1)
                link(nc.vector.tensor_copy(ends_row[:, :, :].rearrange("p c e -> p (c e)"), ps[:, 4, :]))
                link(nc.vector.tensor_copy(ends_sc[:, :, :].rearrange("p j c -> p (j c)"), ps[:, 5, 0:2 * ET]))
                for j in range(JT):
                    link(nc.vector.tensor_scalar(src_node[:, j, :], ends_row[:, 0, :], iota_col[:, j:j + 1], None, ALU.is_equal))
                link(nc.vector.memset(same[:, :], 0.0))
                assert count[0] == GRAPH_NODES

        def set_up(n):
            if n == ENDS_STEP + 1:
                for j in range(ET):
                    last = nc.vector.tensor_scalar(dst_edge[:, j, :], iota_row[:, :], ends_sc[:, j, 1:2], None, ALU.is_equal)
                link(last)
                assert count[0] == GRAPH_EDGES
                dve.wait_ge(graph_pe, 2)
                for j in range(ET):
                    link(nc.vector.tensor_tensor(picked[:, :], ps[:, 4, j * T:(j + 1) * T], dst_edge[:, j, :], ALU.mult))
                    link(nc.vector.reduce_sum(adj_edge[:, j:j + 1], picked[:, :], AX_X))
                link(nc.vector.tensor_scalar(adj_edge[:, :], adj_edge[:, :], EPS_LOG, None, ALU.add))
                assert count[0] == GRAPH_DVE
            if n == ENDS_STEP + 3:
                for j in range(JT):
                    link(nc.vector.tensor_scalar(gather[:, j, 1, :], ends_row[:, 1, :], iota_col[:, j:j + 1], None, ALU.is_equal))
                    link(nc.vector.tensor_tensor(gather[:, j, 0, :], src_node[:, j, :], gather[:, j, 1, :].bitcast(F32), ALU.add))
            if n == ENDS_STEP + 4:
                for j in range(ET):
                    link(nc.vector.tensor_scalar(scatter[:, j, :], iota_row[:, :], ends_sc[:, j, 0:1], None, ALU.is_equal))
                link(nc.vector.tensor_tensor(same[:, 1:E], ends_row[:, 0, 1:E], ends_row[:, 0, 0:E - 1], ALU.is_equal))
                link(nc.vector.tensor_scalar(pen[:, :], same[:, :], BIG, -BIG, ALU.mult, ALU.add))
            if n == ENDS_STEP + 5:
                link(nc.vector.tensor_copy(lin_hi[:, :], lin_raw[:, 0, :]))
                link(nc.vector.tensor_tensor(lin_lo[:, :], lin_raw[:, 0, :], lin_hi[:, :].bitcast(F32), ALU.subtract))
                link(nc.vector.memset(head_pad[:, :, :].bitcast(F32), 0.0))
                link(nc.vector.tensor_copy(head_pad[:, 0, HPAD:], head_raw[:, :]))
                link(nc.vector.tensor_tensor(head_pad[:, 1, HPAD:], head_raw[:, :], head_pad[:, 0, HPAD:].bitcast(F32), ALU.subtract))

        def update(n, st, par, w0=None):
            p, s, nw, slot, f = st["p"], st["s"], st["nw"], st["slot"], st["full"]
            w0 = st["w0"] if w0 is None else w0
            gi, gg, gf, go = (flat(gate[g][par], nw) for g in range(4))
            c = flat(cell[cell_slot(st, par)], nw)
            dve.wait_ge(gate_sb[GATE_I], n + 1)
            dve.wait_ge(gate_sb[GATE_G], n + 1)
            if s == 0:
                nc.vector.tensor_tensor(c, gi, gg, ALU.mult).then_inc(c_ready, 1)
            else:
                nc.vector.tensor_tensor(gg, gi, gg, ALU.mult).then_inc(in_gate, 1)
                dve.wait_ge(gate_sb[GATE_F], f + 1)
                nc.vector.tensor_tensor(gf, gf, c, ALU.mult).then_inc(keep_gate, 1)
                dve.wait_ge(in_gate, f + 1)
                dve.wait_ge(keep_gate, f + 1)
                nc.vector.tensor_tensor(c, gg, gf, ALU.add).then_inc(c_ready, 1)
            dve.wait_ge(tanh_ready, n + 1)
            dve.wait_ge(gate_sb[GATE_O], n + 1)
            nc.vector.tensor_tensor(go, go, flat(tanh_c[par], nw), ALU.mult).then_inc(h_ready, 1)
            dve.wait_ge(h_ready, n + 1)
            if s < p - 1:
                last = nc.vector.tensor_copy(flat(h_rec_hi[slot], nw), go)
            else:
                for h, dst_h in enumerate(halves(windows(hT_hi, p), w0, nw, s)):
                    last = nc.vector.tensor_copy(dst_h, go[:, h, :].rearrange("f (w b) -> f w b", b=HB))
            last.then_inc(h_high, 1)

        lstm_loop(dve, update, before=set_up_first, after=set_up)

        for par in range(2):
            link(nc.vector.memset(head_at[par][:, :, :, :].bitcast(F32), 0.0))

        def graph(i, par):
            if valid(i):
                dve.wait_ge(t_ps, i + 1)
                dve.wait_ge(x_in[par], every_other(i, par) + 16 * NK // 2)
                ge(dve, x1_ready, i - 1)
                nc.vector.tensor_tensor(y[par][:, :, :].rearrange("p g d -> p (g d)"), ps_t,
                                        xs[par][:, :, :, :].rearrange("p b j d -> p (b j d)"), ALU.add).then_inc(y_ready, 1)
            if valid(i - 1):
                dve.wait_ge(std_ready, i)
                nc.vector.reciprocal(rstd[1 - par][:, :], std[1 - par][:, :]).then_inc(rstd_ready, 1)
            if valid(i - 6):
                dve.wait_ge(q_ready, i - 5)
                ge(dve, lr_split, i - 7)
                nc.vector.scalar_tensor_tensor(out=lr[par][:, :, :], in0=qs[par][:, :, :], scalar=SLOPE,
                                               in1=qs[par][:, :, :], op0=ALU.mult, op1=ALU.max).then_inc(lr_ready, 1)
            if valid(i):
                dve.wait_ge(y_ready, i + 1)
                for g in range(2 * JT):
                    last = nc.vector.bn_stats(stat[par][:, g, :], y[par][:, g, :])
                last.then_inc(stats_ready, 1)
            if valid(i - 1):
                dve.wait_ge(rstd_ready, i)
                if valid(i):
                    dve.wait_ge(stats_ready, i + 1)
                dst_rows = x1[:, bass.ds(i - 1, 1)].rearrange("p k g d -> p (k g) d")
                for g in range(2 * JT):
                    last = nc.vector.tensor_scalar(dst_rows[:, g, :], y[1 - par][:, g, :], mv[1 - par][:, g, 0:1],
                                                   rstd[1 - par][:, g:g + 1], ALU.subtract, ALU.mult)
                last.then_inc(x1_ready, 1)
            if valid(i):
                if isinstance(i, int) and i == 0:
                    dve.wait_ge(stats_ready, 1)
                for g in range(2 * JT):
                    last = nc.vector.bn_aggr(mv[par][:, g, :], stat[par][:, g, :])
                last.then_inc(mv_ready, 1)
            if valid(i - 4):
                dve.wait_ge(both_high, i - 3)
                nc.vector.tensor_tensor(both_lo[par][:, :, :], ps_gv[par][:, :, 0:E], both_hi[par][:, :, :].bitcast(F32),
                                        ALU.subtract).then_inc(both_split, 1)
            if valid(i - 7):
                ge(dve, s_ps, i - 8)
                for b in range(2):
                    last = nc.vector.tensor_copy(head_at[1 - par][:, b, :, bass.ds((i - 7) * (2 * NH) + b * NH, HPAD + NH)],
                                                 head_pad[:, :, :])
                last.then_inc(head_ready, 1)
            if isinstance(i, int) and i == 4:
                dve.wait_ge(log_ready, 1)
                dve.wait_ge(consts, 1)
                for j in range(ET):
                    link(nc.vector.tensor_scalar(log_diag[:, j, :], ident[:, :], log_adj[:, j:j + 1], None, ALU.mult))
                link(nc.vector.tensor_copy(log_diag_hi[:, :, :], log_diag[:, :, :]))
                nc.vector.tensor_tensor(log_diag_lo[:, :, :], log_diag[:, :, :], log_diag_hi[:, :, :].bitcast(F32),
                                        ALU.subtract).then_inc(log_ready, 1)

        stages(dve, NK, 7, 10, graph)

        soft = [0]

        def chain(ins):
            soft[0] += 1
            ins.then_inc(soft_dve, 1)
            dve.wait_ge(soft_dve, soft[0])

        dve.wait_ge(s_ps, NK)
        chain(nc.vector.tensor_tensor_scan(run_f[:, :], pen[:, 0:E], ps_s, -BIG, ALU.add, ALU.max))
        chain(nc.vector.tensor_tensor_scan(run_b[:, ::-1], pen[:, E:0:-1], ps_s[:, ::-1], -BIG, ALU.add, ALU.max))
        chain(nc.vector.tensor_tensor(top[:, :], run_f[:, :], run_b[:, :], ALU.max))
        chain(nc.vector.tensor_tensor(top[:, :], ps_s, top[:, :], ALU.subtract))
        assert soft[0] == SOFT_SHIFTED
        dve.wait_ge(soft_act, 1)
        chain(nc.vector.tensor_tensor_scan(run_f[:, :], same[:, 0:E], ex[:, :], 0.0, ALU.mult, ALU.add))
        chain(nc.vector.tensor_tensor_scan(run_b[:, ::-1], same[:, E:0:-1], ex[:, ::-1], 0.0, ALU.mult, ALU.add))
        chain(nc.vector.tensor_tensor(run_b[:, :], run_b[:, :], ex[:, :], ALU.subtract))
        chain(nc.vector.tensor_tensor(den[:, :], run_f[:, :], run_b[:, :], ALU.add))
        chain(nc.vector.reciprocal(rden[:, :], den[:, :]))
        chain(nc.vector.tensor_tensor(weight[:, :], ex[:, :], rden[:, :], ALU.mult))
        assert soft[0] == SOFT_WEIGHT
        dve.wait_ge(soft_pe, 1)
        for j in range(ET):
            chain(nc.vector.tensor_copy(attn[:, :, j, :], ps_t[:, j * BH:(j + 1) * BH].rearrange("p (b h) -> p b h", h=NH)))
        assert soft[0] == SOFT_ATTN
        dve.wait_ge(v_ready, NK)

        attn_k = attn[:, :, :, :].rearrange("p (k b) j h -> p k (b j h)", b=2)

        def rows(i, par):
            if valid(i - 4):
                dve.wait_ge(o_ps, i - 3)
                z = x1[:, bass.ds(i - 4, 1)].rearrange("p k g d -> p (k g) d")
                nc.vector.tensor_tensor(z.rearrange("p g d -> p (g d)"), ps_o[par], z.rearrange("p g d -> p (g d)"),
                                        ALU.add).then_inc(z_ready, 1)
            if valid(i):
                ge(dve, yt_ps, i - 1)
                nc.vector.tensor_tensor(vs[par][:, :, :].rearrange("p g (h d) -> p (g h) d", h=NH),
                                        values[:, bass.ds(i, 1)].rearrange("p k g (h d) -> p (k g h) d", h=NH),
                                        attn_k[:, bass.ds(i, 1), :].rearrange("p k g -> p (k g)").unsqueeze(2)
                                        .to_broadcast([P, 2 * ET * NH, DH]), ALU.mult).then_inc(vs_ready, 1)
            if valid(i - 5):
                dve.wait_ge(zstd_ready, i - 4)
                if valid(i - 4):
                    dve.wait_ge(z_ready, i - 3)
                ge(dve, res_ready, i - 6)
                nc.vector.reciprocal(rstd[1 - par][:, :], std[1 - par][:, :]).then_inc(zrstd_ready, 1)
            if valid(i - 4):
                if isinstance(i, int) and i == 4:
                    dve.wait_ge(z_ready, 1)
                for g in range(2 * JT):
                    last = nc.vector.bn_stats(stat[par][:, g, :], z[:, g, :])
                last.then_inc(zstats_ready, 1)
            if valid(i - 5):
                dve.wait_ge(zrstd_ready, i - 4)
                if valid(i - 4):
                    dve.wait_ge(zstats_ready, i - 3)
                nc.vector.scalar_tensor_tensor(out=shift[1 - par][:, :], in0=mv[1 - par][:, :, 0], scalar=-1.0,
                                               in1=rstd[1 - par][:, :], op0=ALU.mult, op1=ALU.mult).then_inc(zshift_ready, 1)
            if valid(i - 4):
                if isinstance(i, int) and i == 4:
                    dve.wait_ge(zstats_ready, 1)
                for g in range(2 * JT):
                    last = nc.vector.bn_aggr(mv[par][:, g, :], stat[par][:, g, :])
                last.then_inc(zmv_ready, 1)

        stages(dve, NK, 5, 8, rows)

    @block.tensor
    def _(pe):
        def mm(out_, lhsT, rhs, start, stop):
            return nc.tensor.matmul(out_, lhsT, rhs, start=start, stop=stop, skip_group_check=True)

        pe.wait_ge(ones_ready, 1)
        pe.wait_ge(dve_prep, 1)
        terms = [(part, j) for part in (adjT_hi, adjT_lo) for j in range(JT)]
        for n, (part, j) in enumerate(terms):
            last = mm(ps_h2[0][:, 0:T], ones[:, :], part[:, j, :], n == 0, n == len(terms) - 1)
        last.then_inc(pe_prep, 1)

        def adj_product(acc, hi, lo):
            for b in range(2):
                n = 0
                for rows, part in ((hi, adjT_hi), (hi, adjT_lo), (lo, adjT_hi)):
                    for j in range(JT):
                        last = mm(acc[:, b * T:(b + 1) * T], rows[:, b, j, :], part[:, j, :], n == 0, n == 3 * JT - 1)
                        n += 1
            return last

        def first(i, par):
            if valid(i):
                pe.wait_ge(x_split, i + 1)
                ge(pe, z_split, i - 1)
                adj_product(ps_z[par], x_hi[par], x_lo[par]).then_inc(z_ps, 1)
            if valid(i - 1):
                pe.wait_ge(z_split, i)
                if isinstance(i, int) and i == 1:
                    pe.wait_ge(dve_prep, 8)
                ge(pe, h1_ready, i - 2)
                acc = ps_h1[1 - par]
                mm(acc, wg_hi[:, :], z_hi[1 - par][:, :], True, False)
                mm(acc, wg_hi[:, :], z_lo[1 - par][:, :], False, False)
                mm(acc, wg_lo[:, :], z_hi[1 - par][:, :], False, False)
                mm(acc, bias0[:, :], degree[:, :, :].rearrange("p b t -> p (b t)"), False, True).then_inc(h1_ps, 1)
            if valid(i - 2):
                pe.wait_ge(h1_ready, i - 1)
                ge(pe, u_split, i - 3)
                acc = ps_u[par]
                mm(acc, ones[:, :], bias1[:, :].unsqueeze(1).to_broadcast([P, 2 * JT, D]), True, False)
                for g in range(4):
                    c = slice(g * P, (g + 1) * P)
                    last = mm(acc[:, c], h1[par][:, c], layers_raw[:, 1, :], False, g == 3)
                last.then_inc(u_ps, 1)
            if valid(i - 3):
                pe.wait_ge(u_split, i - 2)
                ge(pe, h2_split, i - 4)
                adj_product(ps_h2[1 - par], u_hi[1 - par], u_lo[1 - par]).then_inc(h2_ps, 1)

        stages(pe, NK, 3, 6, first)

        for s in (z_split, h1_ready, u_split, h2_split):
            pe.wait_ge(s, NK)
        pe.wait_ge(wl_split, NK)

        def set_up(n):
            if n == ENDS_STEP:
                pe.wait_ge(graph_dve, GRAPH_ORDER)
                pe.wait_ge(gate_sb[GATE_F], STEPS[n]["full"])
                for c in range(2):
                    for j in range(ET):
                        mm(ps[:, 4, c * E:(c + 1) * E], ends_b[:, j, c, :], order[:, j, :], j == 0, j == ET - 1)
                for r in range(ET):
                    for j in range(ET):
                        last = mm(ps[:, 5, 2 * r:2 * r + 2], order[:, j, r * P:(r + 1) * P].bitcast(F32), ends_c[:, j, :], j == 0, j == ET - 1)
                last.then_inc(graph_pe, 1)
            if n == ROWS_STEP:
                pe.wait_ge(graph_dve, GRAPH_NODES)
                for r in range(ET):
                    for j in range(JT):
                        last = mm(ps[:, 4, r * T:(r + 1) * T], src_node[:, j, r * P:(r + 1) * P], adj_raw[:, j, :], j == 0, j == JT - 1)
                last.then_inc(graph_pe, 1)
            if n == ROWS_STEP + 1:
                pe.wait_ge(graph_dve, GRAPH_DVE)

        PASSES = ((GATE_I, "hi"), (GATE_G, "hi"), (GATE_I, "lo"), (GATE_G, "lo"),
                  (GATE_F, "hi"), (GATE_F, "lo"), (GATE_O, "hi"), (GATE_O, "lo"))
        LOW_FROM = (GATE_I, "lo")
        IN_TURN = tuple((g, part) for g in range(4) for part in ("hi", "lo"))

        def gates(n, st, par, w0=None):
            p, s, nw, slot, f = st["p"], st["s"], st["nw"], st["slot"], st["full"]
            w0 = st["w0"] if w0 is None else w0
            x_parts = {"hi": halves(windows(hT_hi, p), w0, nw, s), "lo": halves(windows(hT_lo, p), w0, nw, s)}
            h_parts = {"hi": [h_rec_hi[slot][:, h, 0:nw * HB] for h in range(2)],
                       "lo": [h_rec_lo[slot][:, h, 0:nw * HB] for h in range(2)]}
            for kind, parts in ((0, x_parts), (1, h_parts)):
                if kind == 1 and s == 0:
                    continue
                need = st["need_x"] if kind == 0 else st["need_h"]
                ge(pe, h_high, need)
                last_kind = kind == (s > 0)
                for g, part in (IN_TURN if p == 1 else PASSES):
                    if g == GATE_F and s == 0:
                        continue
                    if kind == 0 and part == "hi":
                        ge(pe, gate_sb[g], f if g == GATE_F else n)
                    if (g, part) == LOW_FROM:
                        ge(pe, h_split, need)
                    c = slice(GATE_ROW[g] * D, (GATE_ROW[g] + 1) * D)
                    for k, w in enumerate((wl_hi, wl_lo) if part == "hi" else (wl_hi,)):
                        for h in range(2):
                            last = mm(ps[:, 2 * g + h, 0:nw * HB], w[:, kind, p - 1, c], parts[part][h],
                                      kind == 0 and part == "hi" and k == 0, last_kind and part == "lo")
                    if last_kind and part == "lo":
                        last.then_inc(gate_ps[g], 1)

        lstm_loop(pe, gates, before=set_up)

        def rows_of(j, par):
            pe.wait_ge(hs_ready, j + 1)
            ge(pe, y_ready, j)
            for b in range(2):
                for t in range(JT):
                    c = (b * JT + t) * P
                    last = nc.tensor.transpose(ps_t[:, c:c + P], hsum[par][:, b, t * P:(t + 1) * P], ident[:, :])
            last.then_inc(t_ps, 1)

        def graph(i, par):
            if valid(i - 3):
                pe.wait_ge(x1_split, i - 2)
                ge(pe, dst_ready, i - 4)
                ge(pe, both_split, i - 4)
                for b in range(2):
                    n = 0
                    for part in (x1_hi[1 - par], x1_lo[1 - par]):
                        for j in range(JT):
                            last = mm(ps_gv[1 - par][:, b, :], part[:, b * JT + j, :], gather[:, j, :, :].rearrange("p g e -> p (g e)"),
                                      n == 0, n == 2 * JT - 1)
                            n += 1
                last.then_inc(gv_ps, 1)
            if valid(i + 1):
                rows_of(i + 1, 1 - par)
            if isinstance(i, int) and i == 6:
                pe.wait_ge(log_ready, 2)
                for j in range(ET):
                    for part in (log_diag_hi, log_diag_lo):
                        mm(ps_s[:, j * P:(j + 1) * P], ones[:, :], part[:, j, :], j == 0 and part is log_diag_hi, False)
            if valid(i - 8):
                pe.wait_ge(lr_split, i - 7)
                pe.wait_ge(head_ready, i - 7)
                for b in range(2):
                    for part, rhs in ((0, lr_hi[par]), (1, lr_hi[par]), (0, lr_lo[par])):
                        last = mm(ps_s, head_at[par][:, b, part, HPAD:], rhs[:, b, :], False,
                                  isinstance(i, int) and i - 8 == NK - 1 and b == 1 and rhs is lr_lo[par])
                last.then_inc(s_ps, 1)
            if valid(i - 5):
                pe.wait_ge(both_split, i - 4)
                ge(pe, q_ready, i - 5)
                hi, lo = both_hi[1 - par], both_lo[1 - par]
                mm(ps_q, lin_hi[:, :], hi[:, :, :], True, False)
                mm(ps_q, lin_hi[:, :], lo[:, :, :], False, False)
                mm(ps_q, lin_lo[:, :], hi[:, :, :], False, True).then_inc(q_ps, 1)
                pe.wait_ge(dst_ready, i - 4)
                ge(pe, v_ready, i - 5)
                for b in range(2):
                    for j in range(ET):
                        last = mm(ps_v[:, (b * ET + j) * D:(b * ET + j + 1) * D], dst_x[1 - par][:, b, j * P:(j + 1) * P],
                                  lin_raw[:, 1, :], True, True)
                last.then_inc(v_ps, 1)

        for g in range(4):
            pe.wait_ge(gate_sb[g], STEPS[-1]["full"] + 1 if g == GATE_F else NS)
        rows_of(0, 0)
        stages(pe, NK, 8, 10, graph, ahead=1)

        pe.wait_ge(soft_dve, SOFT_WEIGHT)
        for j in range(ET):
            last = nc.tensor.transpose(ps_t[:, j * P:(j + 1) * P], weight[:, j * P:(j + 1) * P], ident[:, :])
        last.then_inc(soft_pe, 1)

        def rows(i, par):
            if valid(i - 1):
                pe.wait_ge(vs_ready, i)
                ge(pe, yt_ready, i - 2)
                for b in range(2):
                    for j in range(ET):
                        last = mm(ps_y[1 - par][:, b * T:(b + 1) * T], vs[1 - par][:, b * ET + j, :], scatter[:, j, :],
                                  j == 0, j == ET - 1)
                last.then_inc(yt_ps, 1)
            if valid(i - 3):
                pe.wait_ge(yt_ready, i - 2)
                ge(pe, z_ready, i - 4)
                for b in range(2):
                    for t in range(JT):
                        g = b * JT + t
                        last = mm(ps_o[1 - par][:, g * D:(g + 1) * D], yt[1 - par][:, b, t * P:(t + 1) * P], lin_raw[:, 2, :], True, True)
                last.then_inc(o_ps, 1)

        stages(pe, NK, 3, 6, rows)

    stacks["all"].close()


def kernel(x, adj, L0_gnn_Wg0, L0_gnn_bg0, L0_gnn_Wg1, L0_gnn_bg1, L0_gnn_Wih, L0_gnn_Whh, L0_gnn_bih, L0_gnn_bhh,
           L1_gnn_W_lin, L1_gnn_W_val, L1_gnn_a, L1_gnn_W_out, L1_gnn_src, L1_gnn_dst):
    import numpy as np
    import concourse.bacc as bacc
    from concourse.bass_utils import run_bass_kernel_spmd

    def arr(v):
        return np.asarray(v)

    def gates_first(b):
        b = arr(b)
        return b.reshape(b.shape[0], 4, -1).transpose(2, 0, 1)

    def rows_at(b, places):
        tile = np.zeros((P, arr(b).shape[0]), arr(b).dtype)
        tile[list(places)] = arr(b)
        return tile

    x = arr(x)
    Bn, T, D = x.shape
    a = arr(L1_gnn_a)
    NH, DH = a.shape
    heads = np.zeros((NH, DH, NH), a.dtype)
    heads[np.arange(NH), :, np.arange(NH)] = a
    heads = heads.reshape(NH * DH, NH)
    JT = T // P
    adj = arr(adj)
    laid = {
        "x": x.reshape(Bn // 2, 2, JT, P, D).transpose(0, 3, 1, 2, 4),
        "adjT": adj.T.reshape(JT, P, T).transpose(1, 0, 2),
        "adj": adj.reshape(JT, P, T).transpose(1, 0, 2),
        "layers": np.stack([arr(L0_gnn_Wg0), arr(L0_gnn_Wg1), rows_at(L0_gnn_bg0, (0, 32, 64)), rows_at(L0_gnn_bg1, (0, 32))], 1),
        "WihT": arr(L0_gnn_Wih).transpose(2, 0, 1), "WhhT": arr(L0_gnn_Whh).transpose(2, 0, 1),
        "bih": gates_first(L0_gnn_bih), "bhh": gates_first(L0_gnn_bhh),
        "linear": np.stack([arr(w).T for w in (L1_gnn_W_lin, L1_gnn_W_val, L1_gnn_W_out)], 1),
        "heads": heads,
        "src": arr(L1_gnn_src)[None],
        "ends": np.stack([arr(L1_gnn_src), arr(L1_gnn_dst)], -1).reshape(-1, P, 2).transpose(1, 0, 2),
    }
    laid = {k: np.ascontiguousarray(v) for k, v in laid.items()}
    nc = bacc.Bacc("TRN2", target_bir_lowering=False, num_devices=1)
    aps = [nc.dram_tensor(f"in_{k}", v.shape, mybir.dt.from_np(v.dtype), kind="ExternalInput").ap() for k, v in laid.items()]
    out = nc.dram_tensor("out", (Bn // 2, P, 2 * JT, D), F32, kind="ExternalOutput").ap()
    build(nc, *aps, out)
    r = run_bass_kernel_spmd(nc, [{f"in_{k}": v for k, v in laid.items()}], core_ids=[0])
    got = r.results[0]["out"]
    return got.reshape(Bn // 2, P, 2, JT, D).transpose(0, 2, 3, 1, 4).reshape(Bn, T, D)
```

```python
from contextlib import ExitStack

import concourse.bass as bass
from concourse import mybir

F32 = mybir.dt.float32
F32R = mybir.dt.float32r
I32 = mybir.dt.int32
ALU = mybir.AluOpType
ACT = mybir.ActivationFunctionType
AX_X = mybir.AxisListType.X

P = 128
BIG = 1e30

GATE_I, GATE_G, GATE_F, GATE_O = range(4)
GATE_ROW = {GATE_I: 0, GATE_F: 1, GATE_G: 2, GATE_O: 3}
GATE_FUNC = {GATE_I: ACT.Sigmoid, GATE_G: ACT.Tanh, GATE_F: ACT.Sigmoid, GATE_O: ACT.Sigmoid}


def lstm_steps(T, skips, job_windows):
    steps = []
    for p in range(1, skips + 1):
        jobs, w = [], 0
        for n in job_windows[p]:
            jobs.append((w, n))
            w += n
        assert w == T // p
        group = {1: 1, 2: 2, 3: len(jobs), 4: len(jobs)}[p]
        for g0 in range(0, len(jobs), group):
            for s in range(p):
                for slot, (w0, nw) in enumerate(jobs[g0:g0 + group]):
                    steps.append(dict(p=p, s=s, w0=w0, nw=nw, slot=slot, group=group,
                                      t0=w0 * p, t1=(w0 + nw) * p))
    full = 0
    for n, st in enumerate(steps):
        st["full"] = full
        full += st["s"] > 0
        need = 0
        for m in range(n):
            o = steps[m]
            if o["s"] == o["p"] - 1 and o["p"] < st["p"] and o["t0"] < st["t1"] and st["t0"] < o["t1"]:
                need = m + 1
        st["need_x"] = need
        st["need_h"] = n - st["group"] + 1
    return steps


def build(nc, x, adjT, adj, layers, WihT, WhhT, bih, bhh, linear, heads, src, ends, out):
    NK = x.shape[0]
    B = 2 * NK
    JT = x.shape[3]
    T = JT * P
    D = x.shape[4]
    SK = WihT.shape[1]
    G4 = 4 * D
    E = src.shape[1]
    ET = E // P
    NH = heads.shape[1]
    DH = D // NH
    BH = B * NH
    HR = BH // 2
    assert (D, T, E, BH, SK) == (P, 2 * P, 2 * P, P, 4)
    PB = 2 * T
    HB = B // 2
    SLOPE, EPS_LN, EPS_LOG = 0.2, 1e-5, 1e-8

    JW = {1: [32] * 8, 2: [32] * 4, 3: [32, 32, 21], 4: [32, 32]}
    STEPS = lstm_steps(T, SK, JW)
    NS = len(STEPS)
    N1 = len(JW[1])
    N2 = len(JW[2])

    stacks = {k: ExitStack() for k in ("all", "states", "whole", "weights", "first", "lstm", "edges", "graph", "rows")}

    def sb(stack, name, shape, dt=F32):
        return stacks[stack].enter_context(nc.sbuf_tensor(name, shape, dt))

    xs = [sb("all", f"xs{i}", [P, 2, JT, D]) for i in range(2)]
    ones = sb("all", "ones", [P, P], F32R)
    lin_raw = sb("all", "lin_raw", [P, 3, D])
    lin_hi = sb("all", "lin_hi", [P, D], F32R)
    lin_lo = sb("all", "lin_lo", [P, D], F32R)
    head_raw = sb("all", "head_raw", [P, NH])
    bias_ih = sb("all", "bias_ih", [P, SK, 4])
    bias_hh = sb("all", "bias_hh", [P, SK, 4])
    bias_gate = sb("all", "bias_gate", [P, SK, 4])
    ident = sb("all", "ident", [P, P])
    iota_row = sb("all", "iota_row", [P, T])
    iota_col = sb("all", "iota_col", [P, JT])
    gather = sb("all", "gather", [P, JT, 2, E], F32R)
    scatter = sb("all", "scatter", [P, ET, T])
    same = sb("all", "same", [P, E + 1])
    pen = sb("all", "pen", [P, E + 1])
    adj_edge = sb("all", "adj_edge", [P, ET])
    log_adj = sb("all", "log_adj", [P, ET])
    eps_ln = sb("all", "eps_ln", [P, 1])
    table_load = sb("all", "table_load", [P, 1])

    hT_hi = sb("states", "hT_hi", [P, T, B], F32R)
    hT_lo = sb("states", "hT_lo", [P, T, B], F32R)

    adj_raw = sb("weights", "adj_raw", [P, JT, T])
    ends_c = sb("weights", "ends_c", [P, ET, 2])
    ends_b = sb("weights", "ends_b", [P, ET, 2, P], F32R)
    order = sb("weights", "order", [P, ET, E], F32R)
    ends_row = sb("weights", "ends_row", [P, 2, E])
    ends_sc = sb("weights", "ends_sc", [P, ET, 2])
    src_node = sb("weights", "src_node", [P, JT, E])
    dst_edge = sb("weights", "dst_edge", [P, ET, T])
    picked = sb("weights", "picked", [P, T])
    wl_hi = sb("weights", "wl_hi", [P, 2, SK, G4], F32R)
    wl_lo = sb("weights", "wl_lo", [P, 2, SK, G4], F32R)

    adjT_hi = sb("first", "adjT_hi", [P, JT, T], F32R)
    adjT_lo = sb("first", "adjT_lo", [P, JT, T], F32R)
    wg_hi = sb("first", "wg_hi", [P, D], F32R)
    wg_lo = sb("first", "wg_lo", [P, D], F32R)
    bias0_deg = sb("first", "bias0_deg", [P, T])
    adjT_raw = sb("first", "adjT_raw", [P, JT, T])
    layers_raw = sb("first", "layers_raw", [P, 3 * D + 1])
    w0_raw, w1_raw, bias1_row = (layers_raw[:, k * D:(k + 1) * D] for k in range(3))
    bias0_col = layers_raw[:, 3 * D:3 * D + 1]
    wl_raw = sb("first", "wl_raw", [P, 2, SK, G4])
    x_hi = [sb("first", f"x_hi{i}", [P, 2, JT, D], F32R) for i in range(2)]
    x_lo = [sb("first", f"x_lo{i}", [P, 2, JT, D], F32R) for i in range(2)]
    z_hi = [sb("first", f"z_hi{i}", [P, PB], F32R) for i in range(2)]
    z_lo = [sb("first", f"z_lo{i}", [P, PB], F32R) for i in range(2)]
    h1 = [sb("first", f"h1_{i}", [P, PB]) for i in range(2)]
    u = [sb("first", f"u{i}", [P, PB]) for i in range(2)]
    u_hi = [sb("first", f"u_hi{i}", [P, 2, JT, D], F32R) for i in range(2)]
    u_lo = [sb("first", f"u_lo{i}", [P, 2, JT, D], F32R) for i in range(2)]
    iota_i = sb("first", "iota_i", [P, T], I32)
    iota_ci = sb("first", "iota_ci", [P, JT], I32)
    ends_i = sb("first", "ends_i", [P, E], I32)
    ends_ci = sb("first", "ends_ci", [P, ET, 2], I32)
    key_row = sb("first", "key_row", [P, E])
    key_col = sb("first", "key_col", [P, ET])
    less = sb("first", "less", [P, ET, E])
    rank = sb("first", "rank", [P, ET])
    stacks["first"].close()

    h_rec_hi = [sb("lstm", f"h_rec_hi{i}", [P, 2, 512], F32R) for i in range(3)]
    h_rec_lo = [sb("lstm", f"h_rec_lo{i}", [P, 2, 512], F32R) for i in range(3)]
    cell = [sb("lstm", f"cell{i}", [P, 2, 512]) for i in range(3)]
    gate = [[sb("lstm", f"gate{g}_{i}", [P, 2, 512]) for i in range(2)] for g in range(4)]
    tanh_c = [sb("lstm", f"tanh_c{i}", [P, 2, 512]) for i in range(2)]
    stacks["lstm"].close()
    stacks["weights"].close()
    stacks["states"].close()
    h_whole = sb("whole", "h_whole", [P, T, B])

    values = sb("edges", "values", [P, NK, 2 * ET, D])
    x1 = sb("edges", "x1", [P, NK, 2 * JT, D])
    attn = sb("edges", "attn", [P, B, ET, NH])
    stat = [sb("edges", f"stat{i}", [P, 2 * JT, 6]) for i in range(2)]
    mv = [sb("edges", f"mv{i}", [P, 2 * JT, 2]) for i in range(2)]
    scores = [sb("edges", f"scores{i}", [P, ET, HR]) for i in range(2)]
    vs = [sb("edges", f"vs{i}", [P, 2 * ET, D]) for i in range(2)]
    std = [sb("edges", f"std{i}", [P, 2 * JT]) for i in range(2)]
    rstd = [sb("edges", f"rstd{i}", [P, 2 * JT]) for i in range(2)]
    shift = [sb("edges", f"shift{i}", [P, 2 * JT]) for i in range(2)]

    h_pair = [sb("graph", f"h_pair{i}", [P, 2, T]) for i in range(2)]
    y = [sb("graph", f"y{i}", [P, 2 * JT, D]) for i in range(2)]
    x1_hi = [sb("graph", f"x1_hi{i}", [P, 2 * JT, D], F32R) for i in range(2)]
    x1_lo = [sb("graph", f"x1_lo{i}", [P, 2 * JT, D], F32R) for i in range(2)]
    both_hi = [sb("graph", f"both_hi{i}", [P, 2, E], F32R) for i in range(2)]
    both_lo = [sb("graph", f"both_lo{i}", [P, 2, E], F32R) for i in range(2)]
    dst_x = [sb("graph", f"dst_x{i}", [P, 2, E]) for i in range(2)]
    qs = [sb("graph", f"qs{i}", [P, 2, E]) for i in range(2)]
    lr = [sb("graph", f"lr{i}", [P, 2, E]) for i in range(2)]
    stacks["graph"].close()

    run_f = sb("rows", "run_f", [HR, E])
    run_b = sb("rows", "run_b", [HR, E])
    top = sb("rows", "top", [HR, E])
    ex = sb("rows", "ex", [HR, E])
    den = sb("rows", "den", [HR, E])
    rden = sb("rows", "rden", [HR, E])
    weight = sb("rows", "weight", [HR, E])
    yt = [sb("rows", f"yt{i}", [P, 2, T]) for i in range(2)]
    res = [sb("rows", f"res{i}", [P, 2 * JT, D]) for i in range(2)]
    res_last = [sb("rows", f"res_last{i}", [P, 2 * JT, D]) for i in range(2)]
    stacks["rows"].close()
    stacks["edges"].close()
    stacks["whole"].close()

    ps = stacks["all"].enter_context(nc.psum_tensor("ps", [P, 8, 512], F32))
    ps_z = [ps[:, i, :] for i in range(2)]
    ps_h1 = [ps[:, 2 + i, :] for i in range(2)]
    ps_u = [ps[:, 4 + i, :] for i in range(2)]
    ps_h2 = [ps[:, 6 + i, :] for i in range(2)]
    ps_gv = [ps[:, 2 * i:2 * i + 2, :] for i in range(2)]
    ps_t = ps[:, 4, :]
    ps_q = ps[:, 5, :]
    ps_v = ps[:, 6, :]
    ps_e = [ps[:, bank, 0:ET * HR].rearrange("p (j c) -> p j c", j=ET) for bank in (7, 4)]
    ps_s = ps[0:HR, 7, E:2 * E]
    ps_a = ps[:, 7, 0:ET * HR]
    ps_y = [ps[:, i, :] for i in range(2)]
    ps_o = [ps[:, 2 + i, :] for i in range(2)]

    def sem(name):
        return stacks["all"].enter_context(nc.semaphore(name))

    adj_in, layers_in, small_in, wl_in, ends_in = (sem(s) for s in ("adj_in", "layers_in", "small_in", "wl_in", "ends_in"))
    x_in = [sem("x_in0"), sem("x_in1")]
    out_done = [sem("out_done0"), sem("out_done1")]
    consts, iotas, ones_ready = sem("consts"), sem("iotas"), sem("ones_ready")
    act_prep, dve_prep, pe_prep, pool_prep = (sem(s) for s in ("act_prep", "dve_prep", "pe_prep", "pool_prep"))
    x_high, x_split = sem("x_high"), sem("x_split")
    z_ps, z_high, z_split = sem("z_ps"), sem("z_high"), sem("z_split")
    h1_ps, h1_sum, h1_ready = sem("h1_ps"), sem("h1_sum"), sem("h1_ready")
    u_ps, u_sum, u_high, u_split = sem("u_ps"), sem("u_sum"), sem("u_high"), sem("u_split")
    h2_ps, h2_high, h2_split = sem("h2_ps"), sem("h2_high"), sem("h2_split")
    wl_high, wl_split = sem("wl_high"), sem("wl_split")
    log_ready, bias_ready = sem("log_ready"), sem("bias_ready")
    graph_dve, graph_pe = sem("graph_dve"), sem("graph_pe")
    gate_ps = [sem(f"gate_ps{g}") for g in range(4)]
    gate_sb = [sem(f"gate_sb{g}") for g in range(4)]
    in_gate, keep_gate, c_ready, tanh_ready = (sem(s) for s in ("in_gate", "keep_gate", "c_ready", "tanh_ready"))
    h_ready, h_high, h_split, last_h = sem("h_ready"), sem("h_high"), sem("h_split"), sem("last_h")
    sum_ready, last_half = sem("sum_ready"), sem("last_half")
    hp_ready, t_ps, y_ready, stats_ready, mv_ready = (sem(s) for s in ("hp_ready", "t_ps", "y_ready", "stats_ready", "mv_ready"))
    std_ready, rstd_ready, x1_ready, x1_high, x1_split = (sem(s) for s in ("std_ready", "rstd_ready", "x1_ready", "x1_high", "x1_split"))
    gv_ps, both_high, dst_ready, both_split = (sem(s) for s in ("gv_ps", "both_high", "dst_ready", "both_split"))
    q_ps, q_ready, lr_ready = sem("q_ps"), sem("q_ready"), sem("lr_ready")
    v_ps, v_ready, s_ps = sem("v_ps"), sem("v_ready"), sem("s_ps")
    soft_dve, soft_act, soft_pe = sem("soft_dve"), sem("soft_act"), sem("soft_pe")
    vs_ready = sem("vs_ready")
    yt_ps, yt_ready = sem("yt_ps"), sem("yt_ready")
    o_ps, z_ready, zstats_ready, zmv_ready = (sem(s) for s in ("o_ps", "z_ready", "zstats_ready", "zmv_ready"))
    zstd_ready, zrstd_ready, zshift_ready, res_ready = (sem(s) for s in ("zstd_ready", "zrstd_ready", "zshift_ready", "res_ready"))

    def ge(eng, s, value):
        if isinstance(value, int) and value <= 0:
            return
        eng.wait_ge(s, value)

    def every_other(j, par):
        return 16 * (j // 2 + 1) if isinstance(j, int) else j * 8 + (16 - 8 * par)

    def stages(eng, n, last, head, body, ahead=0):
        for i in range(head):
            body(i, i % 2)
        stop = n - ahead - (n - ahead - head) % 2
        with eng.Fori(head, stop - 1, 2) as i:
            body(i, head % 2)
            body(i + 1, (head + 1) % 2)
        for i in range(stop, n + last):
            body(i, i % 2)

    def valid(j, n=NK):
        return not isinstance(j, int) or 0 <= j < n

    def halves(view, w0, nw, s):
        return [view[:, bass.ds(w0, nw), s, h * HB:(h + 1) * HB] for h in range(2)]

    def windows(t, p):
        n = T // p
        return t[:, 0:n * p, :].rearrange("f (w s) b -> f w s b", s=p)

    def flat(t, nw):
        return t[:, :, 0:nw * HB]

    def lstm_loop(eng, step, before=None, after=None):
        for n in range(2):
            step(n, STEPS[n], n % 2)
        with eng.Fori(2, N1 - 1, 2) as n:
            for m in range(2):
                step(n + m, STEPS[2 + m], m, w0=(n + m) * JW[1][0])
        with eng.Fori(0, N2 // 2) as q:
            for m in range(4):
                st = STEPS[N1 + m]
                at = dict(st, full=q * 2 + st["full"], need_x=q * 4 + st["need_x"], need_h=q * 4 + st["need_h"])
                step(q * 4 + (N1 + m), at, m % 2, w0=q * (2 * JW[2][0]) + st["w0"])
        for n in range(N1 + 2 * N2, NS):
            if before is not None:
                before(n)
            step(n, STEPS[n], n % 2)
            if after is not None:
                after(n)

    def cell_slot(st, par):
        return par if st["p"] == 1 else st["slot"]

    SCORES_AT = NK
    SHIFT_AT = NK + 1

    KEYS = 5
    GRAPH_ORDER = 2 * ET
    GRAPH_NODES = GRAPH_ORDER + 3 + JT
    GRAPH_EDGES = GRAPH_NODES + 1
    GRAPH_DVE = GRAPH_EDGES + 2 * ET + 1
    SOFT_SCORES = [h * (11 + ET) + 1 for h in range(2)]
    SOFT_SHIFTED = [n + 4 for n in SOFT_SCORES]
    SOFT_WEIGHT = [n + 6 for n in SOFT_SHIFTED]
    SOFT_ATTN = [n + ET for n in SOFT_WEIGHT]

    ENDS_STEP = N1 + 2 * N2
    ROWS_STEP = ENDS_STEP + 2
    assert all(STEPS[n]["s"] == 0 for n in range(ENDS_STEP, ROWS_STEP + 1))

    assert T % SK == 0
    LAST_STEPS = NS - len(JW[SK])
    assert all((st["p"], st["s"]) == (SK, SK - 1) for st in STEPS[LAST_STEPS:])
    SUMS = len(JW[SK]) * (SK - 1)

    block = stacks["all"].enter_context(nc.Block())

    @block.sync
    def _(sp):
        sp.dma_start(adjT_raw[:, :, :], adjT).then_inc(adj_in, 16)

        def load_x(j, par, used, used_count):
            ge(sp, used, used_count)
            sp.dma_start(xs[par][:, :, :, :], x[bass.ds(j, 1)].rearrange("k p b j d -> p (k b) j d")
                         ).then_inc(x_in[par], 16)

        load_x(0, 0, x_split, 0)
        sp.dma_start(layers_raw[:, :], layers).then_inc(layers_in, 16)
        load_x(1, 1, x_split, 0)
        load_x(2, 0, x_split, 1)
        load_x(3, 1, x_split, 2)
        sp.dma_start(wl_raw[:, 0, :, :], WihT).then_inc(wl_in, 16)
        load_x(4, 0, x_split, 3)
        sp.dma_start(wl_raw[:, 1, :, :], WhhT).then_inc(wl_in, 16)
        load_x(5, 1, x_split, 4)
        sp.dma_start(ends_i[:, :], src.broadcast_to([P, E])).then_inc(ends_in, 16)
        sp.dma_start(ends_ci[:, :, :], ends).then_inc(ends_in, 16)
        for t, d in ((bias_ih, bih), (bias_hh, bhh), (lin_raw, linear), (adj_raw, adj)):
            sp.dma_start(t[:, :, :], d).then_inc(small_in, 16)
        sp.dma_start(head_raw[:, :], heads).then_inc(small_in, 16)
        with sp.Fori(6, NK - 1, 2) as j:
            load_x(j, 0, x_split, j - 1)
            load_x(j + 1, 1, x_split, j)
        load_x(0, 0, x_split, NK)
        load_x(1, 1, x_split, NK)
        with sp.Fori(2, NK - 1, 2) as j:
            load_x(j, 0, y_ready, j - 1)
            load_x(j + 1, 1, y_ready, j)

        def store(j, par):
            sp.wait_ge(res_ready, j + 1)
            rows = res[par] if valid(j, NK - 2) else res_last[par]
            sp.dma_start(out[bass.ds(j, 1)].rearrange("k p g d -> p (k g) d"), rows[:, :, :]).then_inc(out_done[par], 16)

        with sp.Fori(0, NK - 3, 2) as j:
            store(j, 0)
            store(j + 1, 1)
        store(NK - 2, 0)
        sp.wait_ge(last_half, 1)
        store(NK - 1, 1)
        for par in range(2):
            sp.wait_ge(out_done[par], 16 * NK // 2)

    @block.gpsimd
    def _(pool):
        nc.gpsimd.memset(ident[:, :], 0.0).then_inc(iotas, 1)
        nc.gpsimd.iota(iota_i[:, :], pattern=[[1, T]], base=0, channel_multiplier=0).then_inc(iotas, 1)
        nc.gpsimd.iota(iota_ci[:, :], pattern=[[P, JT]], base=0, channel_multiplier=1).then_inc(iotas, 1)
        pool.wait_ge(iotas, 3)
        nc.gpsimd.affine_select(out=ident[:, :], in_=ident[:, :], compare_op=ALU.not_equal, fill=1.0,
                                base=0, pattern=[[-1, P]], channel_multiplier=1).then_inc(consts, 1)

        WC = 2 * SK * G4 // NK
        raw = wl_raw[:, :, :, :].rearrange("p a k g -> p (a k g)")
        whi = wl_hi[:, :, :, :].rearrange("p a k g -> p (a k g)")
        wlo = wl_lo[:, :, :, :].rearrange("p a k g -> p (a k g)")

        def first(i, par):
            if valid(i):
                pool.wait_ge(x_high, i + 1)
                nc.gpsimd.tensor_tensor(x_lo[par][:, :, :, :], xs[par][:, :, :, :], x_hi[par][:, :, :, :].bitcast(F32),
                                        ALU.subtract).then_inc(x_split, 1)
            if valid(i - 4):
                pool.wait_ge(wl_in, 16 * 2)
                c = bass.ds((i - 4) * WC, WC)
                nc.gpsimd.tensor_copy(whi[:, c], raw[:, c]).then_inc(wl_high, 1)
                pool.wait_ge(wl_high, i - 3)
                nc.gpsimd.tensor_tensor(wlo[:, c], raw[:, c], whi[:, c].bitcast(F32), ALU.subtract).then_inc(wl_split, 1)

        stages(pool, NK, 4, 6, first)

        keys = [0]

        def link(ins):
            keys[0] += 1
            ins.then_inc(pool_prep, 1)
            pool.wait_ge(pool_prep, keys[0])

        pool.wait_ge(ends_in, 32)
        nc.gpsimd.tensor_copy(iota_row[:, :], iota_i[:, :])
        nc.gpsimd.tensor_copy(iota_col[:, :], iota_ci[:, :])
        nc.gpsimd.tensor_copy(ends_c[:, :, :], ends_ci[:, :, :])
        link(nc.gpsimd.tensor_scalar(key_row[:, :], ends_i[:, :], float(E), None, ALU.mult))
        link(nc.gpsimd.tensor_tensor(key_row[:, :], key_row[:, :], iota_row[:, :], ALU.add))
        link(nc.gpsimd.tensor_scalar(key_col[:, :], ends_c[:, :, 0], float(E), None, ALU.mult))
        link(nc.gpsimd.tensor_tensor(key_col[:, :], key_col[:, :], iota_col[:, :], ALU.add))
        for j in range(ET):
            nc.gpsimd.tensor_scalar(less[:, j, :], key_row[:, :], key_col[:, j:j + 1], None, ALU.is_lt)
            last = nc.gpsimd.tensor_copy(ends_b[:, j, :, :], ends_c[:, j, :].unsqueeze(2).to_broadcast([P, 2, P]))
        link(last)
        assert keys[0] == KEYS

        def h_low(n, st, par, w0=None):
            p, s, nw, slot = st["p"], st["s"], st["nw"], st["slot"]
            w0 = st["w0"] if w0 is None else w0
            if isinstance(n, int) and n >= LAST_STEPS:
                return
            pool.wait_ge(h_high, n + 1)
            o = flat(gate[GATE_O][par], nw)
            if s < p - 1:
                last = nc.gpsimd.tensor_tensor(flat(h_rec_lo[slot], nw), o, flat(h_rec_hi[slot], nw).bitcast(F32), ALU.subtract)
            else:
                his, los = halves(windows(hT_hi, p), w0, nw, s), halves(windows(hT_lo, p), w0, nw, s)
                for h in range(2):
                    last = nc.gpsimd.tensor_tensor(los[h], o[:, h, :].rearrange("f (w b) -> f w b", b=HB),
                                                   his[h].bitcast(F32), ALU.subtract)
            last.then_inc(h_split, 1)
            if p == SK:
                whole, hi, lo = (windows(t, p)[:, w0:w0 + nw, s, :] for t in (h_whole, hT_hi, hT_lo))
                nc.gpsimd.tensor_tensor(whole, hi.bitcast(F32), lo.bitcast(F32), ALU.add).then_inc(sum_ready, 1)

        lstm_loop(pool, h_low)

        def graph(i, par):
            if valid(i - 2):
                pool.wait_ge(x1_high, i - 1)
                nc.gpsimd.tensor_tensor(x1_lo[par][:, :, :], x1[:, bass.ds(i - 2, 1)].rearrange("p k g d -> p (k g) d"),
                                        x1_hi[par][:, :, :].bitcast(F32), ALU.subtract).then_inc(x1_split, 1)

        stages(pool, NK, 2, 4, graph)

        attn_k = attn[:, :, :, :].rearrange("p (k b) j h -> p k (b j h)", b=2)

        def rows(i, par):
            if valid(i):
                ge(pool, yt_ps, i - 1)
                nc.gpsimd.tensor_tensor(vs[par][:, :, :].rearrange("p g (h d) -> p (g h) d", h=NH),
                                        values[:, bass.ds(i, 1)].rearrange("p k g (h d) -> p (k g h) d", h=NH),
                                        attn_k[:, bass.ds(i, 1), :].rearrange("p k g -> p (k g)").unsqueeze(2)
                                        .to_broadcast([P, 2 * ET * NH, DH]), ALU.mult).then_inc(vs_ready, 1)

        pool.wait_ge(soft_dve, SOFT_ATTN[0])
        pool.wait_ge(v_ready, NK // 2)
        rows(0, 0)
        rows(1, 1)
        with pool.Fori(2, NK // 2 - 1, 2) as i:
            rows(i, 0)
            rows(i + 1, 1)
        pool.wait_ge(soft_dve, SOFT_ATTN[1])
        pool.wait_ge(v_ready, NK)
        with pool.Fori(NK // 2, NK - 1, 2) as i:
            rows(i, 0)
            rows(i + 1, 1)

    @block.scalar
    def _(act):
        act.wait_ge(ones_ready, 1)
        nc.scalar.activation(table_load[:, :], ones[:, 0:1].bitcast(F32), ACT.Sigmoid)
        act.wait_ge(adj_in, 16)
        nc.scalar.copy(adjT_hi[:, :, :], adjT_raw[:, :, :]).then_inc(act_prep, 1)

        def x_part(i, par):
            act.wait_ge(x_in[par], every_other(i, par))
            ge(act, z_ps, i - 1)
            nc.scalar.copy(x_hi[par][:, :, :, :], xs[par][:, :, :, :]).then_inc(x_high, 1)

        def first(i, par):
            if isinstance(i, int) and i < 4:
                x_part(i, par)
            if isinstance(i, int) and i == 0:
                act.wait_ge(layers_in, 16)
                nc.scalar.copy(wg_hi[:, :], w0_raw).then_inc(act_prep, 1)
            if valid(i - 1):
                act.wait_ge(z_ps, i)
                nc.scalar.copy(z_hi[1 - par][:, :], ps_z[1 - par]).then_inc(z_high, 1)
            if valid(i) and not (isinstance(i, int) and i < 4):
                x_part(i, par)
            if valid(i - 2):
                act.wait_ge(h1_sum, i - 1)
                nc.scalar.activation(h1[par][:, :], h1[par][:, :], ACT.Relu).then_inc(h1_ready, 1)
            if valid(i - 3):
                act.wait_ge(u_sum, i - 2)
                nc.scalar.copy(u_hi[1 - par][:, :, :, :].rearrange("p b j d -> p (b j d)"), u[1 - par][:, :]).then_inc(u_high, 1)
            if valid(i - 4):
                act.wait_ge(h2_ps, i - 3)
                nc.scalar.activation(hT_hi[:, :, bass.ds((i - 4) * 2, 2)].rearrange("f t b -> f b t"),
                                     ps_h2[par].rearrange("f (b t) -> f b t", b=2), ACT.Relu).then_inc(h2_high, 1)

        stages(act, NK, 4, 6, first)

        def gates(n, st, par, w0=None):
            p, s, nw, slot, f = st["p"], st["s"], st["nw"], st["slot"], st["full"]
            for g in range(4):
                if g == GATE_F and s == 0:
                    continue
                act.wait_ge(gate_ps[g], (f if g == GATE_F else n) + 1)
                ge(act, h_split if g == GATE_O else c_ready, n - 1)
                if g == GATE_O and isinstance(n, int) and n < 2:
                    act.wait_ge(graph_dve, GRAPH_ORDER)
                r = GATE_ROW[g]
                nc.scalar.activation(flat(gate[g][par], nw), ps[:, 2 * g:2 * g + 2, 0:nw * HB], GATE_FUNC[g],
                                     bias=bias_gate[:, p - 1, r:r + 1]).then_inc(gate_sb[g], 1)
                if g == GATE_I:
                    flush()
            pending.append((n, st, par))
            if s > 0:
                flush()

        pending = []

        def flush():
            if pending:
                m, st, par = pending.pop()
                if isinstance(m, int) and m == NS - 1:
                    for h in range(2):
                        act.wait_ge(c_ready, m + 1 + h)
                        nc.scalar.activation(flat(tanh_c[par], st["nw"])[:, h], flat(cell[cell_slot(st, par)], st["nw"])[:, h],
                                             ACT.Tanh).then_inc(tanh_ready, 1)
                    return
                act.wait_ge(c_ready, m + 1)
                nc.scalar.activation(flat(tanh_c[par], st["nw"]), flat(cell[cell_slot(st, par)], st["nw"]),
                                     ACT.Tanh).then_inc(tanh_ready, 1)

        act.wait_ge(bias_ready, 1)
        for n in range(2):
            gates(n, STEPS[n], n % 2)
        with act.Fori(2, N1 - 1, 2) as n:
            pending[:] = [(n - 1, STEPS[1], 1)]
            for m in range(2):
                gates(n + m, STEPS[2 + m], m)
        pending[:] = [(N1 - 1, STEPS[N1 - 1], (N1 - 1) % 2)]
        flush()
        with act.Fori(0, N2 // 2) as q:
            for m in range(4):
                gates(q * 4 + (N1 + m), dict(STEPS[N1 + m], full=q * 2 + STEPS[N1 + m]["full"]), m % 2)
        for n in range(N1 + 2 * N2, NS):
            gates(n, STEPS[n], n % 2)

        def pair_of(j, par):
            ge(act, t_ps, j - 1)
            nc.scalar.copy(h_pair[par][:, :, :], h_whole[:, :, bass.ds(j * 2, 2)].rearrange("f t b -> f b t")
                           ).then_inc(hp_ready, 1)

        act.wait_ge(sum_ready, SUMS)
        act.wait_ge(last_h, len(JW[SK]))
        pair_of(0, 0)
        pair_of(1, 1)
        act.wait_ge(last_h, len(JW[SK]) + 1)

        act.wait_ge(graph_dve, GRAPH_DVE)
        nc.scalar.activation(log_adj[:, :], adj_edge[:, :], ACT.Ln).then_inc(log_ready, 1)

        def exponentials(h):
            act.wait_ge(soft_dve, SOFT_SHIFTED[h])
            nc.scalar.activation(ex[:, :], top[:, :], ACT.Exp).then_inc(soft_act, 1)

        def graph(i, par):
            if valid(i - 6):
                act.wait_ge(q_ps, i - 5)
                ge(act, lr_ready, i - 7)
                nc.scalar.copy(qs[par][:, :, :].rearrange("p b e -> p (b e)"), ps_q).then_inc(q_ready, 1)
                act.wait_ge(v_ps, i - 5)
                nc.scalar.copy(values[:, bass.ds(i - 6, 1)].rearrange("p k g d -> p (k g d)"), ps_v).then_inc(v_ready, 1)
            if isinstance(i, int) and i == SHIFT_AT + 1:
                exponentials(0)
            if valid(i - 2):
                act.wait_ge(x1_ready, i - 1)
                ge(act, gv_ps, i - 3)
                nc.scalar.copy(x1_hi[par][:, :, :], x1[:, bass.ds(i - 2, 1)].rearrange("p k g d -> p (k g) d")).then_inc(x1_high, 1)
            if valid(i + 2):
                pair_of(i + 2, par)
            if valid(i - 4):
                act.wait_ge(gv_ps, i - 3)
                ge(act, v_ps, i - 5)
                nc.scalar.copy(dst_x[par][:, :, :], ps_gv[par][:, :, E:2 * E]).then_inc(dst_ready, 1)
                nc.scalar.copy(both_hi[par][:, :, :], ps_gv[par][:, :, 0:E]).then_inc(both_high, 1)
            if valid(i):
                act.wait_ge(mv_ready, i + 1)
                nc.scalar.activation(std[par][:, :], mv[par][:, :, 1], ACT.Sqrt, bias=eps_ln[:, :]).then_inc(std_ready, 1)

        stages(act, NK, 6, 8, graph, ahead=2)

        exponentials(1)

        def rows(i, par):
            if valid(i - 2):
                act.wait_ge(yt_ps, i - 1)
                ge(act, o_ps, i - 3)
                nc.scalar.copy(yt[par][:, :, :].rearrange("p b t -> p (b t)"), ps_y[par]).then_inc(yt_ready, 1)
            if valid(i - 6):
                act.wait_ge(zshift_ready, i - 5)
                very_last = isinstance(i, int) and i - 6 == NK - 1
                own_slot = isinstance(i, int) and i - 6 >= NK - 2
                to = res_last[par] if own_slot else res[par]
                if not own_slot and not (isinstance(i, int) and i - 6 < 2):
                    act.wait_ge(out_done[par], every_other(i - 8, par))
                at = bass.ds(i - 6, 1)
                for g in range(JT if very_last else 2 * JT):
                    last = nc.scalar.activation(to[:, g, :], x1[:, at, g, :].rearrange("p k d -> p (k d)"), ACT.Identity,
                                                bias=shift[par][:, g:g + 1], scale=rstd[par][:, g:g + 1])
                last.then_inc(res_ready, 1)
            if valid(i - 4):
                act.wait_ge(zmv_ready, i - 3)
                nc.scalar.activation(std[par][:, :], mv[par][:, :, 1], ACT.Sqrt, bias=eps_ln[:, :]).then_inc(zstd_ready, 1)

        stages(act, NK, 6, 8, rows)

    @block.vector
    def _(dve):
        nc.vector.memset(ones[:, :].bitcast(F32), 1.0).then_inc(ones_ready, 1)
        nc.vector.memset(eps_ln[:, :], EPS_LN)
        dve.wait_ge(act_prep, 1)
        nc.vector.tensor_tensor(adjT_lo[:, :, :], adjT_raw[:, :, :], adjT_hi[:, :, :].bitcast(F32), ALU.subtract).then_inc(dve_prep, 1)
        dve.wait_ge(act_prep, 2)
        nc.vector.tensor_tensor(wg_lo[:, :], w0_raw, wg_hi[:, :].bitcast(F32), ALU.subtract).then_inc(dve_prep, 1)
        dve.wait_ge(pe_prep, 1)
        nc.vector.tensor_scalar(bias0_deg[:, :], ps_h2[0][:, 0:T], bias0_col, None, ALU.mult).then_inc(dve_prep, 1)
        dve.wait_ge(dve_prep, 3)

        def h2_low(i, par):
            dve.wait_ge(h2_high, i - 3)
            b2 = bass.ds((i - 4) * 2, 2)
            nc.vector.scalar_tensor_tensor(out=hT_lo[:, :, b2].rearrange("f t b -> f b t"),
                                           in0=ps_h2[par].rearrange("f (b t) -> f b t", b=2), scalar=0.0,
                                           in1=hT_hi[:, :, b2].rearrange("f t b -> f b t").bitcast(F32),
                                           op0=ALU.max, op1=ALU.subtract).then_inc(h2_split, 1)

        def first(i, par):
            if valid(i - 1):
                dve.wait_ge(z_high, i)
                nc.vector.tensor_tensor(z_lo[1 - par][:, :], ps_z[1 - par], z_hi[1 - par][:, :].bitcast(F32),
                                        ALU.subtract).then_inc(z_split, 1)
            if valid(i - 2):
                dve.wait_ge(h1_ps, i - 1)
                ge(dve, u_ps, i - 3)
                nc.vector.tensor_tensor(h1[par][:, :].rearrange("f (b t) -> f b t", b=2), ps_h1[par].rearrange("f (b t) -> f b t", b=2),
                                        bias0_deg[:, :].unsqueeze(1).to_broadcast([P, 2, T]), ALU.add).then_inc(h1_sum, 1)
            if valid(i - 3):
                dve.wait_ge(u_ps, i - 2)
                ge(dve, u_split, i - 4)
                nc.vector.tensor_tensor(u[1 - par][:, :].rearrange("p (g d) -> p g d", d=D), ps_u[1 - par].rearrange("p (g d) -> p g d", d=D),
                                        bias1_row.unsqueeze(1).to_broadcast([P, 2 * JT, D]), ALU.add).then_inc(u_sum, 1)
            if valid(i - 3):
                dve.wait_ge(u_high, i - 2)
                nc.vector.tensor_tensor(u_lo[1 - par][:, :, :, :].rearrange("p b j d -> p (b j d)"), u[1 - par][:, :],
                                        u_hi[1 - par][:, :, :, :].rearrange("p b j d -> p (b j d)").bitcast(F32),
                                        ALU.subtract).then_inc(u_split, 1)
            if valid(i - 4):
                h2_low(i, par)

        stages(dve, NK, 4, 6, first)

        count = [0]

        def link(ins):
            count[0] += 1
            ins.then_inc(graph_dve, 1)
            dve.wait_ge(graph_dve, count[0])

        dve.wait_ge(small_in, 16 * 5)
        nc.vector.tensor_tensor(bias_gate[:, :, :], bias_ih[:, :, :], bias_hh[:, :, :], ALU.add).then_inc(bias_ready, 1)
        dve.wait_ge(pool_prep, KEYS)
        for j in range(ET):
            link(nc.vector.reduce_sum(rank[:, j:j + 1], less[:, j, :], AX_X))
            link(nc.vector.tensor_scalar(order[:, j, :], iota_row[:, :], rank[:, j:j + 1], None, ALU.is_equal))
        assert count[0] == GRAPH_ORDER

        def set_up_first(n):
            if n == ENDS_STEP:
                dve.wait_ge(graph_pe, 1)
                link(nc.vector.tensor_copy(ends_row[:, :, :].rearrange("p c e -> p (c e)"), ps[:, 4, :]))
                link(nc.vector.tensor_copy(ends_sc[:, :, :].rearrange("p j c -> p (j c)"), ps[:, 5, 0:2 * ET]))
                for j in range(JT):
                    link(nc.vector.tensor_scalar(src_node[:, j, :], ends_row[:, 0, :], iota_col[:, j:j + 1], None, ALU.is_equal))
                link(nc.vector.memset(same[:, :], 0.0))
                assert count[0] == GRAPH_NODES

        def set_up_between(n):
            if n == ENDS_STEP:
                for j in range(ET):
                    last = nc.vector.tensor_scalar(dst_edge[:, j, :], iota_row[:, :], ends_sc[:, j, 1:2], None, ALU.is_equal)
                link(last)
                assert count[0] == GRAPH_EDGES
            if n == ENDS_STEP + 1:
                dve.wait_ge(graph_pe, 2)
                for j in range(ET):
                    link(nc.vector.tensor_tensor(picked[:, :], ps[:, 4, j * T:(j + 1) * T], dst_edge[:, j, :], ALU.mult))
                    link(nc.vector.reduce_sum(adj_edge[:, j:j + 1], picked[:, :], AX_X))
                link(nc.vector.tensor_scalar(adj_edge[:, :], adj_edge[:, :], EPS_LOG, None, ALU.add))
                assert count[0] == GRAPH_DVE

        def set_up(n):
            if n == ENDS_STEP + 3:
                for j in range(JT):
                    link(nc.vector.tensor_scalar(gather[:, j, 1, :], ends_row[:, 1, :], iota_col[:, j:j + 1], None, ALU.is_equal))
                    link(nc.vector.tensor_tensor(gather[:, j, 0, :], src_node[:, j, :], gather[:, j, 1, :].bitcast(F32), ALU.add))
            if n == ENDS_STEP + 4:
                for j in range(ET):
                    link(nc.vector.tensor_scalar(scatter[:, j, :], iota_row[:, :], ends_sc[:, j, 0:1], None, ALU.is_equal))
                link(nc.vector.tensor_tensor(same[:, 1:E], ends_row[:, 0, 1:E], ends_row[:, 0, 0:E - 1], ALU.is_equal))
                link(nc.vector.tensor_scalar(pen[:, :], same[:, :], BIG, -BIG, ALU.mult, ALU.add))
            if n == ENDS_STEP + 5:
                link(nc.vector.tensor_copy(lin_hi[:, :], lin_raw[:, 0, :]))
                link(nc.vector.tensor_tensor(lin_lo[:, :], lin_raw[:, 0, :], lin_hi[:, :].bitcast(F32), ALU.subtract))

        def last_updates(n, f, gi, gg, gf, go, c, th, dst):
            parts = [slice(0, 1), slice(1, 2)] if n == NS - 1 else [slice(0, 2)]
            nc.vector.tensor_tensor(gg, gi, gg, ALU.mult).then_inc(in_gate, 1)
            dve.wait_ge(gate_sb[GATE_F], f + 1)
            nc.vector.tensor_tensor(gf, gf, c, ALU.mult).then_inc(keep_gate, 1)
            dve.wait_ge(in_gate, f + 1)
            dve.wait_ge(keep_gate, f + 1)
            for h in parts:
                nc.vector.tensor_tensor(c[:, h], gg[:, h], gf[:, h], ALU.add).then_inc(c_ready, 1)
            dve.wait_ge(gate_sb[GATE_O], n + 1)
            for k, h in enumerate(parts):
                dve.wait_ge(tanh_ready, n + 1 + k)
                for q in range(h.start, h.stop):
                    last = nc.vector.tensor_tensor(dst[q], go[:, q].rearrange("f (w b) -> f w b", b=HB),
                                                   th[:, q].rearrange("f (w b) -> f w b", b=HB), ALU.mult)
                last.then_inc(last_h, 1)

        def update(n, st, par, w0=None):
            p, s, nw, slot, f = st["p"], st["s"], st["nw"], st["slot"], st["full"]
            w0 = st["w0"] if w0 is None else w0
            gi, gg, gf, go = (flat(gate[g][par], nw) for g in range(4))
            c = flat(cell[cell_slot(st, par)], nw)
            dve.wait_ge(gate_sb[GATE_I], n + 1)
            dve.wait_ge(gate_sb[GATE_G], n + 1)
            if isinstance(n, int) and n >= LAST_STEPS:
                last_updates(n, f, gi, gg, gf, go, c, flat(tanh_c[par], nw), halves(windows(h_whole, p), w0, nw, s))
                return
            if s == 0:
                nc.vector.tensor_tensor(c, gi, gg, ALU.mult).then_inc(c_ready, 1)
                if isinstance(n, int):
                    set_up_between(n)
            else:
                nc.vector.tensor_tensor(gg, gi, gg, ALU.mult).then_inc(in_gate, 1)
                dve.wait_ge(gate_sb[GATE_F], f + 1)
                nc.vector.tensor_tensor(gf, gf, c, ALU.mult).then_inc(keep_gate, 1)
                dve.wait_ge(in_gate, f + 1)
                dve.wait_ge(keep_gate, f + 1)
                nc.vector.tensor_tensor(c, gg, gf, ALU.add).then_inc(c_ready, 1)
            dve.wait_ge(tanh_ready, n + 1)
            dve.wait_ge(gate_sb[GATE_O], n + 1)
            nc.vector.tensor_tensor(go, go, flat(tanh_c[par], nw), ALU.mult).then_inc(h_ready, 1)
            dve.wait_ge(h_ready, n + 1)
            if s < p - 1:
                last = nc.vector.tensor_copy(flat(h_rec_hi[slot], nw), go)
            else:
                for h, dst_h in enumerate(halves(windows(hT_hi, p), w0, nw, s)):
                    last = nc.vector.tensor_copy(dst_h, go[:, h, :].rearrange("f (w b) -> f w b", b=HB))
            last.then_inc(h_high, 1)

        lstm_loop(dve, update, before=set_up_first, after=set_up)

        soft = [0]

        def chain(ins):
            soft[0] += 1
            ins.then_inc(soft_dve, 1)
            dve.wait_ge(soft_dve, soft[0])

        def row_scores(h):
            dve.wait_ge(s_ps, (h + 1) * NK // 2)
            dve.wait_ge(log_ready, 1)
            for j in range(ET):
                last = nc.vector.tensor_scalar(scores[h][:, j, :], ps_e[h][:, j, :], log_adj[:, j:j + 1], None, ALU.add)
            chain(last)
            assert soft[0] == SOFT_SCORES[h]

        def maxima(h):
            dve.wait_ge(soft_pe, 2 * h + 1)
            chain(nc.vector.tensor_tensor_scan(run_f[:, :], pen[0:HR, 0:E], ps_s, -BIG, ALU.add, ALU.max))
            chain(nc.vector.tensor_tensor_scan(run_b[:, ::-1], pen[0:HR, E:0:-1], ps_s[:, ::-1], -BIG, ALU.add, ALU.max))
            chain(nc.vector.tensor_tensor(top[:, :], run_f[:, :], run_b[:, :], ALU.max))
            chain(nc.vector.tensor_tensor(top[:, :], ps_s, top[:, :], ALU.subtract))
            assert soft[0] == SOFT_SHIFTED[h]

        def exp_sums(h):
            dve.wait_ge(soft_act, h + 1)
            chain(nc.vector.tensor_tensor_scan(run_f[:, :], same[0:HR, 0:E], ex[:, :], 0.0, ALU.mult, ALU.add))
            chain(nc.vector.tensor_tensor_scan(run_b[:, ::-1], same[0:HR, E:0:-1], ex[:, ::-1], 0.0, ALU.mult, ALU.add))
            chain(nc.vector.tensor_tensor(run_b[:, :], run_b[:, :], ex[:, :], ALU.subtract))
            chain(nc.vector.tensor_tensor(den[:, :], run_f[:, :], run_b[:, :], ALU.add))

        def reciprocals(h):
            chain(nc.vector.reciprocal(rden[:, :], den[:, :]))

        def weights(h):
            chain(nc.vector.tensor_tensor(weight[:, :], ex[:, :], rden[:, :], ALU.mult))
            assert soft[0] == SOFT_WEIGHT[h]

        def attn_of(h):
            dve.wait_ge(soft_pe, 2 * h + 2)
            for j in range(ET):
                chain(nc.vector.tensor_copy(attn[:, h * HB:(h + 1) * HB, j, :],
                                            ps_a[:, j * HR:(j + 1) * HR].rearrange("p (b h) -> p b h", h=NH)))
            assert soft[0] == SOFT_ATTN[h]

        def graph(i, par):
            if valid(i):
                dve.wait_ge(t_ps, i + 1)
                dve.wait_ge(x_in[par], every_other(i, par) + 16 * NK // 2)
                ge(dve, x1_ready, i - 1)
                nc.vector.tensor_tensor(y[par][:, :, :].rearrange("p g d -> p (g d)"), ps_t,
                                        xs[par][:, :, :, :].rearrange("p b j d -> p (b j d)"), ALU.add).then_inc(y_ready, 1)
            if valid(i - 1):
                dve.wait_ge(std_ready, i)
                nc.vector.reciprocal(rstd[1 - par][:, :], std[1 - par][:, :]).then_inc(rstd_ready, 1)
            if valid(i - 6):
                dve.wait_ge(q_ready, i - 5)
                ge(dve, s_ps, i - 7)
                nc.vector.scalar_tensor_tensor(out=lr[par][:, :, :], in0=qs[par][:, :, :], scalar=SLOPE,
                                               in1=qs[par][:, :, :], op0=ALU.mult, op1=ALU.max).then_inc(lr_ready, 1)
            if valid(i):
                dve.wait_ge(y_ready, i + 1)
                for g in range(2 * JT):
                    last = nc.vector.bn_stats(stat[par][:, g, :], y[par][:, g, :])
                last.then_inc(stats_ready, 1)
            if valid(i - 1):
                dve.wait_ge(rstd_ready, i)
                dst_rows = x1[:, bass.ds(i - 1, 1)].rearrange("p k g d -> p (k g) d")
                for g in range(2 * JT):
                    if g == 2 * JT - 1 and valid(i):
                        dve.wait_ge(stats_ready, i + 1)
                    last = nc.vector.tensor_scalar(dst_rows[:, g, :], y[1 - par][:, g, :], mv[1 - par][:, g, 0:1],
                                                   rstd[1 - par][:, g:g + 1], ALU.subtract, ALU.mult)
                last.then_inc(x1_ready, 1)
            if valid(i):
                if isinstance(i, int) and i == 0:
                    dve.wait_ge(stats_ready, 1)
                for g in range(2 * JT):
                    last = nc.vector.bn_aggr(mv[par][:, g, :], stat[par][:, g, :])
                last.then_inc(mv_ready, 1)
            if valid(i - 4):
                dve.wait_ge(both_high, i - 3)
                nc.vector.tensor_tensor(both_lo[par][:, :, :], ps_gv[par][:, :, 0:E], both_hi[par][:, :, :].bitcast(F32),
                                        ALU.subtract).then_inc(both_split, 1)
            for at, part in ((SCORES_AT, row_scores), (SHIFT_AT, maxima), (SHIFT_AT + 1, exp_sums),
                             (SHIFT_AT + 2, reciprocals), (SHIFT_AT + 3, weights)):
                if isinstance(i, int) and i == at:
                    part(0)

        stages(dve, NK, 6, 8, graph)

        attn_of(0)
        for part in (row_scores, maxima, exp_sums, reciprocals, weights, attn_of):
            part(1)


        def rows(i, par):
            if valid(i - 4):
                dve.wait_ge(o_ps, i - 3)
                z = x1[:, bass.ds(i - 4, 1)].rearrange("p k g d -> p (k g) d")
                nc.vector.tensor_tensor(z.rearrange("p g d -> p (g d)"), ps_o[par], z.rearrange("p g d -> p (g d)"),
                                        ALU.add).then_inc(z_ready, 1)
            if valid(i - 5):
                dve.wait_ge(zstd_ready, i - 4)
                if valid(i - 4):
                    dve.wait_ge(z_ready, i - 3)
                ge(dve, res_ready, i - 6)
                nc.vector.reciprocal(rstd[1 - par][:, :], std[1 - par][:, :]).then_inc(zrstd_ready, 1)
            if valid(i - 4):
                if isinstance(i, int) and i == 4:
                    dve.wait_ge(z_ready, 1)
                for g in range(2 * JT):
                    last = nc.vector.bn_stats(stat[par][:, g, :], z[:, g, :])
                last.then_inc(zstats_ready, 1)
            if valid(i - 5):
                dve.wait_ge(zrstd_ready, i - 4)
                if valid(i - 4):
                    dve.wait_ge(zstats_ready, i - 3)
                nc.vector.scalar_tensor_tensor(out=shift[1 - par][:, :], in0=mv[1 - par][:, :, 0], scalar=-1.0,
                                               in1=rstd[1 - par][:, :], op0=ALU.mult, op1=ALU.mult).then_inc(zshift_ready, 1)
            if valid(i - 4):
                if isinstance(i, int) and i == 4:
                    dve.wait_ge(zstats_ready, 1)
                for g in range(2 * JT):
                    last = nc.vector.bn_aggr(mv[par][:, g, :], stat[par][:, g, :])
                last.then_inc(zmv_ready, 1)

        stages(dve, NK, 5, 8, rows)
        dve.wait_ge(zshift_ready, NK)
        for g in range(JT, 2 * JT):
            last = nc.vector.tensor_scalar(res_last[1][:, g, :], x1[:, NK - 1, g, :], rstd[1][:, g:g + 1], shift[1][:, g:g + 1],
                                           ALU.mult, ALU.add)
        last.then_inc(last_half, 1)

    @block.tensor
    def _(pe):
        def mm(out_, lhsT, rhs, start, stop):
            return nc.tensor.matmul(out_, lhsT, rhs, start=start, stop=stop, skip_group_check=True)

        pe.wait_ge(ones_ready, 1)
        pe.wait_ge(dve_prep, 1)
        terms = [(part, j) for part in (adjT_hi, adjT_lo) for j in range(JT)]
        for n, (part, j) in enumerate(terms):
            last = mm(ps_h2[0][:, 0:T], ones[:, :], part[:, j, :], n == 0, n == len(terms) - 1)
        last.then_inc(pe_prep, 1)

        def adj_product(acc, hi, lo):
            for b in range(2):
                n = 0
                for rows, part in ((hi, adjT_hi), (hi, adjT_lo), (lo, adjT_hi)):
                    for j in range(JT):
                        last = mm(acc[:, b * T:(b + 1) * T], rows[:, b, j, :], part[:, j, :], n == 0, n == 3 * JT - 1)
                        n += 1
            return last

        def first(i, par):
            if valid(i):
                pe.wait_ge(x_split, i + 1)
                ge(pe, z_split, i - 1)
                adj_product(ps_z[par], x_hi[par], x_lo[par]).then_inc(z_ps, 1)
            if valid(i - 1):
                pe.wait_ge(z_split, i)
                if isinstance(i, int) and i == 1:
                    pe.wait_ge(dve_prep, 3)
                ge(pe, h1_sum, i - 2)
                acc = ps_h1[1 - par]
                mm(acc, wg_hi[:, :], z_hi[1 - par][:, :], True, False)
                mm(acc, wg_hi[:, :], z_lo[1 - par][:, :], False, False)
                mm(acc, wg_lo[:, :], z_hi[1 - par][:, :], False, True).then_inc(h1_ps, 1)
            if valid(i - 2):
                pe.wait_ge(h1_ready, i - 1)
                ge(pe, u_sum, i - 3)
                acc = ps_u[par]
                for g in range(4):
                    c = slice(g * P, (g + 1) * P)
                    last = mm(acc[:, c], h1[par][:, c], w1_raw, True, True)
                last.then_inc(u_ps, 1)
            if valid(i - 3):
                pe.wait_ge(u_split, i - 2)
                ge(pe, h2_split, i - 4)
                adj_product(ps_h2[1 - par], u_hi[1 - par], u_lo[1 - par]).then_inc(h2_ps, 1)

        stages(pe, NK, 3, 6, first)

        for s in (z_split, h1_sum, u_sum, h2_high):
            pe.wait_ge(s, NK)
        pe.wait_ge(wl_split, NK)

        def set_up(n):
            if n == ENDS_STEP:
                pe.wait_ge(graph_dve, GRAPH_ORDER)
                pe.wait_ge(gate_sb[GATE_F], STEPS[n]["full"])
                for c in range(2):
                    for j in range(ET):
                        mm(ps[:, 4, c * E:(c + 1) * E], ends_b[:, j, c, :], order[:, j, :], j == 0, j == ET - 1)
                for r in range(ET):
                    for j in range(ET):
                        last = mm(ps[:, 5, 2 * r:2 * r + 2], order[:, j, r * P:(r + 1) * P].bitcast(F32), ends_c[:, j, :], j == 0, j == ET - 1)
                last.then_inc(graph_pe, 1)
            if n == ROWS_STEP:
                pe.wait_ge(graph_dve, GRAPH_NODES)
                for r in range(ET):
                    for j in range(JT):
                        last = mm(ps[:, 4, r * T:(r + 1) * T], src_node[:, j, r * P:(r + 1) * P], adj_raw[:, j, :], j == 0, j == JT - 1)
                last.then_inc(graph_pe, 1)

        PASSES = ((GATE_I, "hi"), (GATE_G, "hi"), (GATE_I, "lo"), (GATE_G, "lo"),
                  (GATE_F, "hi"), (GATE_F, "lo"), (GATE_O, "hi"), (GATE_O, "lo"))
        LOW_FROM = (GATE_I, "lo")
        IN_TURN = tuple((g, part) for g in range(4) for part in ("hi", "lo"))

        def gates(n, st, par, w0=None):
            p, s, nw, slot, f = st["p"], st["s"], st["nw"], st["slot"], st["full"]
            w0 = st["w0"] if w0 is None else w0
            x_parts = {"hi": halves(windows(hT_hi, p), w0, nw, s), "lo": halves(windows(hT_lo, p), w0, nw, s)}
            h_parts = {"hi": [h_rec_hi[slot][:, h, 0:nw * HB] for h in range(2)],
                       "lo": [h_rec_lo[slot][:, h, 0:nw * HB] for h in range(2)]}
            for kind, parts in ((0, x_parts), (1, h_parts)):
                if kind == 1 and s == 0:
                    continue
                need = st["need_x"] if kind == 0 else st["need_h"]
                ge(pe, h_high, need)
                last_kind = kind == (s > 0)
                for g, part in (IN_TURN if p == 1 else PASSES):
                    if g == GATE_F and s == 0:
                        continue
                    if kind == 0 and part == "hi":
                        ge(pe, gate_sb[g], f if g == GATE_F else n)
                        if g == GATE_F and isinstance(n, int) and n == ROWS_STEP + 1:
                            pe.wait_ge(graph_dve, GRAPH_DVE)
                    if isinstance(n, int) and n == 0 and (g, part) == LOW_FROM:
                        pe.wait_ge(h2_split, NK)
                    if (g, part) == LOW_FROM:
                        ge(pe, h_split, need)
                    c = slice(GATE_ROW[g] * D, (GATE_ROW[g] + 1) * D)
                    for k, w in enumerate((wl_hi, wl_lo) if part == "hi" else (wl_hi,)):
                        for h in range(2):
                            last = mm(ps[:, 2 * g + h, 0:nw * HB], w[:, kind, p - 1, c], parts[part][h],
                                      kind == 0 and part == "hi" and k == 0, last_kind and part == "lo")
                    if last_kind and part == "lo":
                        last.then_inc(gate_ps[g], 1)

        lstm_loop(pe, gates, before=set_up)

        def rows_of(j, par):
            pe.wait_ge(hp_ready, j + 1)
            ge(pe, y_ready, j)
            for b in range(2):
                for t in range(JT):
                    c = (b * JT + t) * P
                    last = nc.tensor.transpose(ps_t[:, c:c + P], h_pair[par][:, b, t * P:(t + 1) * P], ident[:, :])
            last.then_inc(t_ps, 1)

        def graph(i, par):
            if valid(i - 3):
                pe.wait_ge(x1_split, i - 2)
                ge(pe, dst_ready, i - 4)
                ge(pe, both_split, i - 4)
                for b in range(2):
                    n = 0
                    for part in (x1_hi[1 - par], x1_lo[1 - par]):
                        for j in range(JT):
                            last = mm(ps_gv[1 - par][:, b, :], part[:, b * JT + j, :], gather[:, j, :, :].rearrange("p g e -> p (g e)"),
                                      n == 0, n == 2 * JT - 1)
                            n += 1
                last.then_inc(gv_ps, 1)
            if valid(i + 1):
                rows_of(i + 1, 1 - par)
            if valid(i - 7):
                pe.wait_ge(lr_ready, i - 6)
                half = int(isinstance(i, int) and i - 7 >= NK // 2)
                if half:
                    pe.wait_ge(y_ready, NK)
                for b in range(2):
                    for j in range(ET):
                        last = mm(ps_e[half][:, j, bass.ds((i - 7 - half * (NK // 2)) * (2 * NH) + b * NH, NH)],
                                  lr[1 - par][:, b, j * P:(j + 1) * P], head_raw[:, :], True, True)
                last.then_inc(s_ps, 1)
            if valid(i - 5):
                pe.wait_ge(both_split, i - 4)
                ge(pe, q_ready, i - 5)
                hi, lo = both_hi[1 - par], both_lo[1 - par]
                mm(ps_q, lin_hi[:, :], hi[:, :, :], True, False)
                mm(ps_q, lin_hi[:, :], lo[:, :, :], False, False)
                mm(ps_q, lin_lo[:, :], hi[:, :, :], False, True).then_inc(q_ps, 1)
                pe.wait_ge(dst_ready, i - 4)
                ge(pe, v_ready, i - 5)
                for b in range(2):
                    for j in range(ET):
                        last = mm(ps_v[:, (b * ET + j) * D:(b * ET + j + 1) * D], dst_x[1 - par][:, b, j * P:(j + 1) * P],
                                  lin_raw[:, 1, :], True, True)
                last.then_inc(v_ps, 1)
            if isinstance(i, int) and i == SHIFT_AT:
                turn_scores(0)
            if isinstance(i, int) and i == SHIFT_AT + 4:
                turn_weights(0)

        def turn_scores(h):
            pe.wait_ge(soft_dve, SOFT_SCORES[h])
            for j in range(ET):
                last = nc.tensor.transpose(ps_s[:, j * P:(j + 1) * P], scores[h][:, j, :], ident[:, :])
            last.then_inc(soft_pe, 1)

        def turn_weights(h):
            pe.wait_ge(soft_dve, SOFT_WEIGHT[h])
            for j in range(ET):
                last = nc.tensor.transpose(ps_a[:, j * HR:(j + 1) * HR], weight[:, j * P:(j + 1) * P], ident[0:HR, 0:HR])
            last.then_inc(soft_pe, 1)

        for g in range(4):
            pe.wait_ge(gate_sb[g], STEPS[-1]["full"] + 1 if g == GATE_F else NS)
        rows_of(0, 0)
        stages(pe, NK, 7, 10, graph, ahead=1)

        turn_scores(1)

        def rows(i, par):
            if valid(i - 1):
                pe.wait_ge(vs_ready, i)
                ge(pe, yt_ready, i - 2)
                for b in range(2):
                    for j in range(ET):
                        last = mm(ps_y[1 - par][:, b * T:(b + 1) * T], vs[1 - par][:, b * ET + j, :], scatter[:, j, :],
                                  j == 0, j == ET - 1)
                last.then_inc(yt_ps, 1)
            if valid(i - 3):
                pe.wait_ge(yt_ready, i - 2)
                ge(pe, z_ready, i - 4)
                for b in range(2):
                    for t in range(JT):
                        g = b * JT + t
                        last = mm(ps_o[1 - par][:, g * D:(g + 1) * D], yt[1 - par][:, b, t * P:(t + 1) * P], lin_raw[:, 2, :], True, True)
                last.then_inc(o_ps, 1)
            if isinstance(i, int) and i == 3:
                turn_weights(1)

        stages(pe, NK, 3, 6, rows)

    stacks["all"].close()


def kernel(x, adj, L0_gnn_Wg0, L0_gnn_bg0, L0_gnn_Wg1, L0_gnn_bg1, L0_gnn_Wih, L0_gnn_Whh, L0_gnn_bih, L0_gnn_bhh,
           L1_gnn_W_lin, L1_gnn_W_val, L1_gnn_a, L1_gnn_W_out, L1_gnn_src, L1_gnn_dst):
    import numpy as np
    import concourse.bacc as bacc
    from concourse.bass_utils import run_bass_kernel_spmd

    def arr(v):
        return np.asarray(v)

    def gates_first(b):
        b = arr(b)
        return b.reshape(b.shape[0], 4, -1).transpose(2, 0, 1)

    x = arr(x)
    Bn, T, D = x.shape
    a = arr(L1_gnn_a)
    NH, DH = a.shape
    heads = np.zeros((NH, DH, NH), a.dtype)
    heads[np.arange(NH), :, np.arange(NH)] = a
    heads = heads.reshape(NH * DH, NH)
    JT = T // P
    adj = arr(adj)
    laid = {
        "x": x.reshape(Bn // 2, 2, JT, P, D).transpose(0, 3, 1, 2, 4),
        "adjT": adj.T.reshape(JT, P, T).transpose(1, 0, 2),
        "adj": adj.reshape(JT, P, T).transpose(1, 0, 2),
        "layers": np.concatenate([arr(L0_gnn_Wg0), arr(L0_gnn_Wg1), np.broadcast_to(arr(L0_gnn_bg1), (D, D)),
                                  arr(L0_gnn_bg0)[:, None]], 1),
        "WihT": arr(L0_gnn_Wih).transpose(2, 0, 1), "WhhT": arr(L0_gnn_Whh).transpose(2, 0, 1),
        "bih": gates_first(L0_gnn_bih), "bhh": gates_first(L0_gnn_bhh),
        "linear": np.stack([arr(w).T for w in (L1_gnn_W_lin, L1_gnn_W_val, L1_gnn_W_out)], 1),
        "heads": heads,
        "src": arr(L1_gnn_src)[None],
        "ends": np.stack([arr(L1_gnn_src), arr(L1_gnn_dst)], -1).reshape(-1, P, 2).transpose(1, 0, 2),
    }
    laid = {k: np.ascontiguousarray(v) for k, v in laid.items()}
    nc = bacc.Bacc("TRN2", target_bir_lowering=False, num_devices=1)
    aps = [nc.dram_tensor(f"in_{k}", v.shape, mybir.dt.from_np(v.dtype), kind="ExternalInput").ap() for k, v in laid.items()]
    out = nc.dram_tensor("out", (Bn // 2, P, 2 * JT, D), F32, kind="ExternalOutput").ap()
    build(nc, *aps, out)
    r = run_bass_kernel_spmd(nc, [{f"in_{k}": v for k, v in laid.items()}], core_ids=[0])
    got = r.results[0]["out"]
    return got.reshape(Bn // 2, P, 2, JT, D).transpose(0, 2, 3, 1, 4).reshape(Bn, T, D)
```
